# Optimizing a Trainium2 kernel written in Bass

```python
import numpy as np
import jax
import jax.numpy as jnp

def _softmax(x, axis=-1):
    return jax.nn.softmax(x, axis=axis)

def _gelu(x):
    return jax.nn.gelu(x, approximate=True)

def _silu(x):
    return jax.nn.silu(x)

def _sigmoid(x):
    return jax.nn.sigmoid(x)

def _layernorm(x, axis=-1, eps=1e-05):
    m = jnp.mean(x, axis=axis, keepdims=True)
    v = jnp.var(x, axis=axis, keepdims=True)
    return (x - m) / jnp.sqrt(v + eps)

def _scatter_add(tgt, idx, src, axis=0):
    return tgt.at[idx].add(src)

def _segment_sum(src, seg, n):
    return jax.ops.segment_sum(src, seg, n)
kernel_name = 'mk_macaron_d2_jaxref_r8_5182d2'

def setup_inputs(seed: int=0):
    np.random.seed(seed)
    _w = jnp.asarray

    def _L0_attn_setup():
        import jax, jax.numpy as jnp
        import numpy as np
        import math
        NUM_HEADS = 16
        ROPE_BASE = 10000.0

        def _rope_cos_sin(seq_len, head_dim, dtype):
            half = head_dim // 2
            inv_freq = 1.0 / ROPE_BASE ** (jnp.arange(0, head_dim, 2, dtype=jnp.float32) / head_dim)
            t = jnp.arange(seq_len, dtype=jnp.float32)
            freqs = jnp.einsum('i,j->ij', t, inv_freq)
            cos = jnp.cos(freqs).astype(dtype)[None, None]
            sin = jnp.sin(freqs).astype(dtype)[None, None]
            return (cos, sin)

        def _apply_rope(x, cos, sin):
            half = x.shape[-1] // 2
            x1, x2 = (x[..., :half], x[..., half:])
            return jnp.concatenate([x1 * cos - x2 * sin, x2 * cos + x1 * sin], axis=-1)
        key = jax.random.key(seed)
        ks = jax.random.split(key, 5)
        B, S, H = (2, 256, 256)
        scale = 1.0 / math.sqrt(H)
        return {'hidden_states': jax.random.normal(ks[0], (B, S, H), dtype=jnp.float32), 'Wq': jax.random.normal(ks[1], (H, H), dtype=jnp.float32) * scale, 'Wk': jax.random.normal(ks[2], (H, H), dtype=jnp.float32) * scale, 'Wv': jax.random.normal(ks[3], (H, H), dtype=jnp.float32) * scale, 'Wo': jax.random.normal(ks[4], (H, H), dtype=jnp.float32) * scale}
    _L0_attn_in = _L0_attn_setup()

    def _L0_ffn_setup():
        import jax, jax.numpy as jnp
        import numpy as np
        L, N, E, H, K = (256, 8, 256, 1024, 8)
        key = jax.random.key(seed)
        ks = jax.random.split(key, 6)
        return {'x': jax.random.normal(ks[0], (L, N, E), dtype=jnp.float32), 'proj1': jax.random.normal(ks[1], (H, E), dtype=jnp.float32) * 0.02, 'proj1_bias': jax.random.normal(ks[2], (H,), dtype=jnp.float32) * 0.02, 'proj2': jax.random.normal(ks[3], (E, H), dtype=jnp.float32) * 0.02, 'proj2_bias': jax.random.normal(ks[4], (E,), dtype=jnp.float32) * 0.02, 'gate_w': jax.random.normal(ks[5], (E, K), dtype=jnp.float32)}
    _L0_ffn_in = _L0_ffn_setup()

    def _L1_attn_setup():
        import jax, jax.numpy as jnp
        import numpy as np
        B, S, HID = (2, 256, 256)
        NH, NKV, HD = (16, 4, 128)
        KV_DIM = NKV * HD
        key = jax.random.key(seed)
        ks = jax.random.split(key, 7)
        sc = 0.02
        return {'hidden_states': jax.random.normal(ks[0], (B, S, HID), dtype=jnp.float32), 'Wq': jax.random.normal(ks[1], (NH * HD, HID), dtype=jnp.float32) * sc, 'Wk': jax.random.normal(ks[2], (KV_DIM, HID), dtype=jnp.float32) * sc, 'Wv': jax.random.normal(ks[3], (KV_DIM, HID), dtype=jnp.float32) * sc, 'Wo': jax.random.normal(ks[4], (HID, NH * HD), dtype=jnp.float32) * sc, 'bo': jnp.zeros((HID,), dtype=jnp.float32)}
    _L1_attn_in = _L1_attn_setup()

    def _L1_ffn_setup():
        import jax, jax.numpy as jnp
        import numpy as np
        N_BLOCKS = 6
        DIM = 256
        HIDDEN = 4 * DIM
        LN_EPS = 1e-05
        W_SCALE = 0.02

        def _block(x, w1, b1, w2, b2):
            h = jax.nn.gelu(jnp.einsum('bsd,hd->bsh', x, w1) + b1, approximate=False)
            return jnp.einsum('bsh,dh->bsd', h, w2) + b2 + x

        def _layernorm(x, g, b):
            mu = jnp.mean(x, axis=-1, keepdims=True)
            var = jnp.mean(jnp.square(x - mu), axis=-1, keepdims=True)
            return (x - mu) * jax.lax.rsqrt(var + LN_EPS) * g + b
        key = jax.random.key(seed)
        ks = jax.random.split(key, 4)
        x = jax.random.normal(ks[0], (4, 256, DIM), dtype=jnp.float32)
        W1 = jax.random.normal(ks[1], (N_BLOCKS, HIDDEN, DIM), dtype=jnp.float32) * W_SCALE
        B1 = jnp.zeros((N_BLOCKS, HIDDEN), dtype=jnp.float32)
        W2 = jax.random.normal(ks[2], (N_BLOCKS, DIM, HIDDEN), dtype=jnp.float32) * W_SCALE
        B2 = jnp.zeros((N_BLOCKS, DIM), dtype=jnp.float32)
        LN_G = jnp.ones((N_BLOCKS - 1, DIM), dtype=jnp.float32)
        LN_B = jnp.zeros((N_BLOCKS - 1, DIM), dtype=jnp.float32)
        return {'x': x, 'W1': W1, 'B1': B1, 'W2': W2, 'B2': B2, 'LN_G': LN_G, 'LN_B': LN_B}
    _L1_ffn_in = _L1_ffn_setup()
    _d = {'L0_attn_hidden_states': _L0_attn_in['hidden_states'], 'L0_attn_Wq': _L0_attn_in['Wq'], 'L0_attn_Wk': _L0_attn_in['Wk'], 'L0_attn_Wv': _L0_attn_in['Wv'], 'L0_attn_Wo': _L0_attn_in['Wo'], 'L0_ffn_proj1': _L0_ffn_in['proj1'], 'L0_ffn_proj1_bias': _L0_ffn_in['proj1_bias'], 'L0_ffn_proj2': _L0_ffn_in['proj2'], 'L0_ffn_proj2_bias': _L0_ffn_in['proj2_bias'], 'L0_ffn_gate_w': _L0_ffn_in['gate_w'], 'L1_attn_Wq': _L1_attn_in['Wq'], 'L1_attn_Wk': _L1_attn_in['Wk'], 'L1_attn_Wv': _L1_attn_in['Wv'], 'L1_attn_Wo': _L1_attn_in['Wo'], 'L1_attn_bo': _L1_attn_in['bo'], 'L1_ffn_W1': _L1_ffn_in['W1'], 'L1_ffn_B1': _L1_ffn_in['B1'], 'L1_ffn_W2': _L1_ffn_in['W2'], 'L1_ffn_B2': _L1_ffn_in['B2'], 'L1_ffn_LN_G': _L1_ffn_in['LN_G'], 'L1_ffn_LN_B': _L1_ffn_in['LN_B']}
    _x0 = _d['L0_attn_hidden_states']
    _d['L0_attn_hidden_states'] = jax.random.normal(jax.random.fold_in(jax.random.key(seed), 1), (2, 1024, 256), dtype=_x0.dtype)
    del _x0
    return _d

def reference(L0_attn_hidden_states, L0_attn_Wq, L0_attn_Wk, L0_attn_Wv, L0_attn_Wo, L0_ffn_proj1, L0_ffn_proj1_bias, L0_ffn_proj2, L0_ffn_proj2_bias, L0_ffn_gate_w, L1_attn_Wq, L1_attn_Wk, L1_attn_Wv, L1_attn_Wo, L1_attn_bo, L1_ffn_W1, L1_ffn_B1, L1_ffn_W2, L1_ffn_B2, L1_ffn_LN_G, L1_ffn_LN_B):

    def _L0_attn_ref(hidden_states, Wq, Wk, Wv, Wo):
        import jax, jax.numpy as jnp
        import numpy as np
        import math
        NUM_HEADS = 16
        ROPE_BASE = 10000.0

        def _rope_cos_sin(seq_len, head_dim, dtype):
            half = head_dim // 2
            inv_freq = 1.0 / ROPE_BASE ** (jnp.arange(0, head_dim, 2, dtype=jnp.float32) / head_dim)
            t = jnp.arange(seq_len, dtype=jnp.float32)
            freqs = jnp.einsum('i,j->ij', t, inv_freq)
            cos = jnp.cos(freqs).astype(dtype)[None, None]
            sin = jnp.sin(freqs).astype(dtype)[None, None]
            return (cos, sin)

        def _apply_rope(x, cos, sin):
            half = x.shape[-1] // 2
            x1, x2 = (x[..., :half], x[..., half:])
            return jnp.concatenate([x1 * cos - x2 * sin, x2 * cos + x1 * sin], axis=-1)
        B, S, H = hidden_states.shape
        nh = NUM_HEADS
        hd = H // nh

        def proj(W):
            y = jnp.einsum('bsh,oh->bso', hidden_states, W)
            return y.reshape(B, S, nh, hd).transpose(0, 2, 1, 3)
        q, k, v = (proj(Wq), proj(Wk), proj(Wv))
        cos, sin = _rope_cos_sin(S, hd, hidden_states.dtype)
        q = _apply_rope(q, cos, sin)
        k = _apply_rope(k, cos, sin)
        scores = jnp.einsum('bhqd,bhkd->bhqk', q, k) / math.sqrt(hd)
        causal = jnp.triu(jnp.full((S, S), -jnp.inf, dtype=scores.dtype), k=1)
        scores = scores + causal[None, None]
        probs = jax.nn.softmax(scores, axis=-1)
        ctx = jnp.einsum('bhqk,bhkd->bhqd', probs, v)
        ctx = ctx.transpose(0, 2, 1, 3).reshape(B, S, H)
        out = jnp.einsum('bsh,oh->bso', ctx, Wo)
        return out

    def _L0_ffn_ref(x, proj1, proj1_bias, proj2, proj2_bias, gate_w):
        import jax, jax.numpy as jnp
        import numpy as np
        L, N, E, H, K = (256, 8, 256, 1024, 8)
        dst = jnp.argmax(jnp.einsum('lne,ek->lnk', x, gate_w), axis=-1)
        h = jax.nn.gelu(jnp.einsum('lne,he->lnh', x, proj1) + proj1_bias, approximate=False)
        out = jnp.einsum('lnh,eh->lne', h, proj2) + proj2_bias
        del dst
        return out

    def _L1_attn_ref(hidden_states, Wq, Wk, Wv, Wo, bo):
        import jax, jax.numpy as jnp
        import numpy as np
        B, S, HID = (2, 256, 256)
        NH, NKV, HD = (16, 4, 128)
        KV_DIM = NKV * HD
        b, s, _ = hidden_states.shape
        q = (hidden_states @ Wq.T).reshape(b, s, NH, HD).transpose(0, 2, 1, 3)
        k = (hidden_states @ Wk.T).reshape(b, s, NKV, HD).transpose(0, 2, 1, 3)
        v = (hidden_states @ Wv.T).reshape(b, s, NKV, HD).transpose(0, 2, 1, 3)
        g = NH // NKV
        k_rep = jnp.repeat(k, g, axis=1)
        v_rep = jnp.repeat(v, g, axis=1)
        qf = q.astype(jnp.float32)
        kf = k_rep.astype(jnp.float32)
        scores = jnp.einsum('bhqd,bhkd->bhqk', qf, kf)
        causal = jnp.tril(jnp.ones((s, s), dtype=bool))[None, None]
        neg = jnp.finfo(scores.dtype).min
        scores = jnp.where(causal, scores, neg)
        attn = jax.nn.softmax(scores, axis=-1).astype(v.dtype)
        out = jnp.einsum('bhqk,bhkd->bhqd', attn, v_rep)
        out = out.transpose(0, 2, 1, 3).reshape(b, s, NH * HD)
        return out @ Wo.T + bo

    def _L1_ffn_ref(x, W1, B1, W2, B2, LN_G, LN_B):
        import jax, jax.numpy as jnp
        import numpy as np
        N_BLOCKS = 6
        DIM = 256
        HIDDEN = 4 * DIM
        LN_EPS = 1e-05
        W_SCALE = 0.02

        def _block(x, w1, b1, w2, b2):
            h = jax.nn.gelu(jnp.einsum('bsd,hd->bsh', x, w1) + b1, approximate=False)
            return jnp.einsum('bsh,dh->bsd', h, w2) + b2 + x

        def _layernorm(x, g, b):
            mu = jnp.mean(x, axis=-1, keepdims=True)
            var = jnp.mean(jnp.square(x - mu), axis=-1, keepdims=True)
            return (x - mu) * jax.lax.rsqrt(var + LN_EPS) * g + b
        for i in range(N_BLOCKS):
            x = _block(x, W1[i], B1[i], W2[i], B2[i])
            if i < N_BLOCKS - 1:
                x = _layernorm(x, LN_G[i], LN_B[i])
        return x
    x = L0_attn_hidden_states
    x = x + 0.5 * _L0_ffn_ref(_layernorm(x, axis=-1), L0_ffn_proj1, L0_ffn_proj1_bias, L0_ffn_proj2, L0_ffn_proj2_bias, L0_ffn_gate_w)
    x = x + _L0_attn_ref(_layernorm(x, axis=-1), L0_attn_Wq, L0_attn_Wk, L0_attn_Wv, L0_attn_Wo)
    x = x + 0.5 * _L0_ffn_ref(_layernorm(x, axis=-1), L0_ffn_proj1, L0_ffn_proj1_bias, L0_ffn_proj2, L0_ffn_proj2_bias, L0_ffn_gate_w)
    x = x + 0.5 * _L1_ffn_ref(_layernorm(x, axis=-1), L1_ffn_W1, L1_ffn_B1, L1_ffn_W2, L1_ffn_B2, L1_ffn_LN_G, L1_ffn_LN_B)
    x = x + _L1_attn_ref(_layernorm(x, axis=-1), L1_attn_Wq, L1_attn_Wk, L1_attn_Wv, L1_attn_Wo, L1_attn_bo)
    x = x + 0.5 * _L1_ffn_ref(_layernorm(x, axis=-1), L1_ffn_W1, L1_ffn_B1, L1_ffn_W2, L1_ffn_B2, L1_ffn_LN_G, L1_ffn_LN_B)
    return x

_drawn_inputs = setup_inputs


def setup_inputs(seed=0):
    import zlib

    import numpy as np

    out = dict(_drawn_inputs(seed))
    spreads = {'L1_attn_bo': (0.0, 0.1),
     'L1_ffn_B1': (0.0, 0.1),
     'L1_ffn_B2': (0.0, 0.1),
     'L1_ffn_LN_G': (1.0, 0.2),
     'L1_ffn_LN_B': (0.0, 0.1)}
    factors = {'L0_ffn_proj1_bias': 7.437}
    for name, (base, spread) in spreads.items():
        noise = np.random.default_rng([zlib.crc32(name.encode()), seed]).standard_normal(out[name].shape)
        drawn = base * np.exp(spread * noise) if base else spread * noise
        out[name] = jnp.asarray(drawn.astype(out[name].dtype))
    for name, factor in factors.items():
        out[name] = (out[name] * factor).astype(out[name].dtype)
    return out
```

```python
from contextlib import ExitStack

import concourse.bass as bass
import numpy as np
from concourse import mybir
from concourse.alu_op_type import AluOpType as ALU

PART = 128
BATCH, SEQ, DIM = 2, 1024, 256
TOKENS = BATCH * SEQ
HIDDEN = 1024
BLOCKS = 6
CHUNK = 512
CHUNKS = TOKENS // CHUNK
TILES = TOKENS // PART
TPC = CHUNK // PART
KD = DIM // PART
HT = HIDDEN // PART
EPS = 1e-5
HEADS = 16
HD0 = DIM // HEADS
HD1 = 128
KV1 = 4
GROUP = 4
GROUPS = BATCH * HEADS // GROUP
QT = SEQ // PART
ROPE_BASE = 10000.0
MASKED = -1e30
RSQRT_GUESS = 0x5F3759DF
A0_W = 5 * KD * DIM + GROUP * DIM
A1_W = 10 * DIM
A1_MISC = 4 + GROUP * 6
FFN_BLOCKS = (1, 1, BLOCKS, BLOCKS)
LAG = 2
PARTS = ((1, 0), (0, 1), (0, 0))


PRE = (0, 1, 3)


def build(nc, a, LASTK=3, FINAL=True, ATTS=(0, 1)):
    f32, f32r, i32, bf16 = mybir.dt.float32, mybir.dt.float32r, mybir.dt.int32, mybir.dt.bfloat16
    ACT = mybir.ActivationFunctionType
    AX = mybir.AxisListType
    ctx = ExitStack()
    with ctx:
        def sb(name, shape, dt=f32, stack=ctx):
            return stack.enter_context(nc.sbuf_tensor(name, shape, dt))

        def sem(name):
            return ctx.enter_context(nc.semaphore(name))

        x = sb("x", [PART, TILES, DIM])
        xT = sb("xT", [PART, 2, KD, TOKENS], f32r)
        xb = sb("xb", [PART, TILES, DIM])
        rb = sb("rb", [PART, TPC, DIM])
        xn = sb("xn", [PART, TPC, DIM])
        xTf = sb("xTf", [PART, KD, CHUNK])
        rows = sb("rows", [PART, 1 + 2 * BLOCKS, DIM])
        B2_0, BO, B2_1, GAIN = 0, 1, 2, 2 + BLOCKS
        lnb = sb("lnb", [PART, BLOCKS - 1, DIM])
        b1 = sb("b1", [PART, (1 + BLOCKS) * HT])
        gT = sb("gT", [PART, BLOCKS * KD])
        bT = sb("bT", [PART, BLOCKS * KD])
        ident = sb("ident", [PART, PART])
        stats = sb("stats", [PART, TPC, 6])
        mv = sb("mv", [PART, TPC, 2])
        var = sb("var", [PART, TPC])
        rstd = sb("rstd", [PART, TPC])
        nt = sb("nt", [PART, TPC])
        negmax = sb("negmax", [PART, QT])
        rowsum = sb("rowsum", [PART, QT])
        rowinv = sb("rowinv", [PART, QT])
        ident_b = sb("ident_b", [PART, PART], bf16)
        mask_b = sb("mask_b", [PART, PART], bf16)

        ffn = ExitStack()
        wraw = sb("wraw", [PART, 2, KD * HIDDEN], f32, ffn)
        w = [sb(f"w{p}", [PART, 2, 2, KD * HIDDEN], f32r, ffn) for p in range(2)]
        gel = sb("gel", [PART, 4, CHUNK], f32, ffn)
        hid = sb("hid", [PART, 2, 4, CHUNK], f32r, ffn)
        ffn.close()

        att = ExitStack()
        p_lo = sb("p_lo", [PART, TPC, SEQ // 2], f32, att)
        p_hi = sb("p_hi", [PART, TPC, SEQ], f32, att)
        pT = sb("pT", [PART, 2, 2, CHUNK], f32r, att)
        ctxT = sb("ctxT", [PART, 2, SEQ], f32r, att)
        q_sb = sb("q_sb", [PART, 2, 2, SEQ], f32r, att)
        k_sb = sb("k_sb", [PART, 2, SEQ], f32r, att)
        v_sb = sb("v_sb", [PART, 2, QT, HD1], f32r, att)
        w_a1 = sb("w_a1", [PART, 2, A1_W], f32r, att)
        att.close()
        att = ExitStack()
        for name, shape in (("p_lo0", [PART, TPC, SEQ // 2]), ("p_hi0", [PART, TPC, SEQ])):
            sb(name, shape, f32, att)
        sb("pT0", [PART, 2, 2, CHUNK], f32r, att)
        sb("ctxT0", [PART, 2, SEQ], f32r, att)
        q_st = sb("q_st", [64, 2, SEQ], f32r, att)
        k_st = sb("k_st", [64, 2, SEQ], f32r, att)
        v_st = sb("v_st", [PART, QT, PART], f32r, att)
        w_a0 = sb("w_a0", [PART, 2, A0_W], f32r, att)
        att.close()
        att = ExitStack()
        rot = sb("rot", [PART, 4, SEQ], f32, att)
        rope = sb("rope", [PART, 3, 2, CHUNK], f32, att)
        rope_hl = sb("rope_hl", [PART, 2, 2, CHUNK], f32r, att)
        v_hl = sb("v_hl", [PART, 2, HEADS, 2, HD0], f32r, att)
        att.close()

        qk_dram = nc.dram_tensor("qk_dram", (2, DIM, 2, TOKENS), f32, kind="Internal").ap()
        v_dram = nc.dram_tensor("v_dram", (TILES, PART, 2 * DIM), f32, kind="Internal").ap()
        ps = ctx.enter_context(nc.psum_tensor("ps", [PART, 8, CHUNK], f32))
        HPS, YPS, TPS = 0, 4, 6
        y_ps = ps[:, YPS:YPS + 2, :].rearrange("p b (t e) -> p (b t) e", e=DIM)

        in_loaded = sem("in_loaded")
        lnb_loaded = sem("lnb_loaded")
        tab_ready = sem("tab_ready")
        rows_ready = sem("rows_ready")
        w_loaded = sem("w_loaded")
        w_high = sem("w_high")
        w_split = sem("w_split")
        hid_ready = sem("hid_ready")
        gelu_done = sem("gelu_done")
        round_done = sem("round_done")
        low_done = sem("low_done")
        mm2_done = sem("mm2_done")
        y_free = sem("y_free")
        x_updated = sem("x_updated")
        xn_ready = sem("xn_ready")
        tr_ready = sem("tr_ready")
        aff_done = sem("aff_done")
        xTh_done = sem("xTh_done")
        xT_ready = sem("xT_ready")
        xb_scaled = sem("xb_scaled")
        xb_ready = sem("xb_ready")
        dve_link = sem("dve_link")
        out_stored = sem("out_stored")
        att_tab = sem("att_tab")
        ident_ready = sem("ident_ready")
        a_loaded = sem("a_loaded")
        a_high = sem("a_high")
        a_low = sem("a_low")
        proj_ready = sem("proj_ready")
        rope_term = sem("rope_term")
        rope_taken = sem("rope_taken")
        rope_sum = sem("rope_sum")
        rope_high = sem("rope_high")
        rope_low = sem("rope_low")
        v_ready = sem("v_ready")
        v_high = sem("v_high")
        v_low = sem("v_low")
        v_loaded = sem("v_loaded")
        s_ready = sem("s_ready")
        max_ready = sem("max_ready")
        exp_done = sem("exp_done")
        inv_ready = sem("inv_ready")
        p_ready = sem("p_ready")
        pt_ready = sem("pt_ready")
        pt_high = sem("pt_high")
        pt_low = sem("pt_low")
        av_done = sem("av_done")
        ctx_high = sem("ctx_high")
        ctx_low = sem("ctx_low")
        out_ready = sem("out_ready")
        out_added = sem("out_added")
        misc_ready = sem("misc_ready")
        misc_high = sem("misc_high")
        misc_free = sem("misc_free")
        vt_ready = sem("vt_ready")
        vt_high = sem("vt_high")
        vt_low = sem("vt_low")
        w1_loaded = sem("w1_loaded")
        w1_high = sem("w1_high")
        w1_split = sem("w1_split")
        rope_stored = [sem(f"rope_stored_{s}") for s in range(2)]
        v_stored = [sem(f"v_stored_{s}") for s in range(2)]
        qk_loaded = [sem(f"qk_loaded_{s}") for s in range(2)]

        class At:
            pass

        def phase(k):
            p = At()
            p.k, p.blocks, p.l1 = k, FFN_BLOCKS[k], FFN_BLOCKS[k] > 1
            p.g0, p.n0 = CHUNKS * sum(FFN_BLOCKS[:k]), sum(FFN_BLOCKS[:k])
            p.pre = k in PRE
            p.s0 = p.g0 + CHUNKS * sum(j in PRE for j in range(k + 1))
            p.tab = 1 if p.l1 else 0
            p.xb0 = CHUNKS * BLOCKS if k == 3 else 0
            p.last = "final" if k == 3 else "last"
            return p

        def walk(p, engine, step):
            def at(blk, c, par, kind):
                return p.g0 + CHUNKS * blk + c, p.s0 + CHUNKS * blk + c, c, blk, par, kind

            def block_steps(blk, par, kind, before):
                prev = None
                if before:
                    prev = at(blk - 1, CHUNKS - 1, 1 - par, before)
                step(at(blk, 0, par, kind), prev)
                with engine.Fori(1, CHUNKS) as c:
                    step(at(blk, c, par, kind), at(blk, c - 1, par, kind))

            par0, last = p.n0 % 2, p.blocks - 1
            block_steps(0, par0, p.last if last == 0 else "inner", None)
            if p.blocks > 1:
                with engine.Fori(0, (p.blocks - 2) // 2) as i:
                    block_steps(1 + 2 * i, 1 - par0, "inner", "inner")
                    block_steps(2 + 2 * i, par0, "inner", "inner")
                block_steps(last, (par0 + last) % 2, p.last, "inner")

        def tail(p):
            return (p.g0 + CHUNKS * p.blocks - 1, p.s0 + CHUNKS * p.blocks - 1, CHUNKS - 1,
                    p.blocks - 1, 0, p.last)

        def positive(v):
            return not isinstance(v, int) or v > 0

        def wait(e, semaphore, v):
            if positive(v):
                e.wait_ge(semaphore, v)

        def wait_apart(e, *waits):
            for _, v in waits:
                if not isinstance(v, int):
                    e.compute_val(v)
            e.wait_ge(in_loaded, 16 * N_IN)
            for semaphore, v in waits:
                wait(e, semaphore, v)

        def pe_transpose_chunk(pe, s):
            pe.wait_ge(xn_ready, s + 1)
            wait(pe, aff_done, s)
            for k in range(KD):
                for t in range(TPC):
                    last = nc.tensor.transpose(ps[:, TPS + k, t * PART:(t + 1) * PART],
                                               xn[:, t, k * PART:(k + 1) * PART], ident[:])
            last.then_inc(tr_ready, 1)

        def pe_step(pe, p, at, prev):
            g, s, c, blk, par, kind = at
            pe.wait_ge(w_split, 4 * (p.n0 + blk + 1))
            pe.wait_ge(xT_ready, s - CHUNKS + 1)

            def mm1(j):
                wait(pe, gelu_done, HT * g + j + 1 - 4)
                first = True
                for wp, xp in PARTS:
                    for k in range(KD):
                        last = nc.tensor.matmul(
                            ps[:, HPS + j % 4, :],
                            w[par][:, wp, 0, k * HIDDEN + j * PART:k * HIDDEN + (j + 1) * PART],
                            xT[:, xp, k, bass.ds(c * CHUNK, CHUNK)], start=first,
                            stop=(wp, xp) == (0, 0) and k == KD - 1)
                        first = False
                last.then_inc(hid_ready, 1)

            def mm2(j):
                if j == 0:
                    wait(pe, y_free, g)
                pe.wait_ge(low_done, HT * g + j + 1)
                for t in range(TPC):
                    for n, (hp, wp) in enumerate(PARTS):
                        last = nc.tensor.matmul(
                            y_ps[:, t, :], hid[:, hp, j % 4, t * PART:(t + 1) * PART],
                            w[par][:, wp, 1, j * DIM:(j + 1) * DIM],
                            start=j == 0 and n == 0 and t % 2 == 0, stop=j == HT - 1 and n == 2,
                            skip_group_check=True)
                last.then_inc(mm2_done, 1)

            for j in range(HT + LAG):
                if j < HT:
                    mm1(j)
                if j >= LAG:
                    mm2(j - LAG)
                if j == 4 and prev is not None and prev[5] != "final":
                    pe_transpose_chunk(pe, prev[1])

        def act_affine(act, s, c, row):
            wait_apart(act, (tr_ready, s + 1),
                       (xT_ready, s))
            for k in range(KD):
                last = nc.scalar.activation(xTf[:, k, :], ps[:, TPS + k, :], ACT.Identity,
                                            bias=bT[:, bass.ds(row * KD + k, 1)],
                                            scale=gT[:, bass.ds(row * KD + k, 1)])
            last.then_inc(aff_done, 1)
            wait_apart(act, (aff_done, s + 1))
            nc.scalar.activation(xT[:, 0, :, bass.ds(c * CHUNK, CHUNK)], xTf[:], ACT.Copy)\
                .then_inc(xTh_done, 1)

        def act_step(act, p, at, prev):
            g, s, c, blk, par, kind = at

            def gelu(j):
                wait_apart(act, (hid_ready, HT * g + j + 1),
                           (low_done, HT * g + j + 1 - 4))
                nc.scalar.activation(gel[:, j % 4, :], ps[:, HPS + j % 4, :], ACT.Gelu,
                                     bias=b1[:, bass.ds((p.tab + blk) * HT + j, 1)]).then_inc(gelu_done, 1)

            def high(j):
                act.wait_ge(gelu_done, HT * g + j + 1)
                wait(act, mm2_done, HT * g + j + 1 - 4)
                nc.scalar.activation(hid[:, 0, j % 4, :], gel[:, j % 4, :], ACT.Copy).then_inc(round_done, 1)

            for j in range(HT + 1):
                if j < HT:
                    gelu(j)
                if j >= 1:
                    high(j - 1)
                if j == 5 and prev is not None and prev[5] != "final":
                    act_affine(act, prev[1], prev[2], prev[3] + 1 if prev[5] == "inner" else 0)

        NORM_LINKS = 14

        def dve_take(dve, p, at):
            g, s, c, blk, par, kind = at
            tiles = bass.ds(c * TPC, TPC)
            dve.wait_ge(mm2_done, HT * g + HT)
            if p.l1:
                dve.wait_ge(xb_ready, p.xb0 + CHUNKS * blk + c + 1)
                add = xb[:, tiles, :]
            else:
                add = rows[:, B2_0:B2_0 + 1, :].broadcast_to([PART, TPC, DIM])
            nc.vector.tensor_tensor(rb[:], y_ps[:, :, :], add, ALU.add).then_inc(y_free, 1)
            dve.wait_ge(y_free, g + 1)
            if kind != "inner":
                nc.vector.scalar_tensor_tensor(x[:, tiles, :], rb[:], 0.5, x[:, tiles, :], ALU.mult, ALU.add)\
                    .then_inc(x_updated, 1)
                wait_apart(dve, (x_updated, CHUNKS * p.k + c + 1 + (CHUNKS if p.k == 3 else 0)))

        def dve_norm(dve, s, c, inner, xb_made):
            n = [0]

            def link(ins):
                n[0] += 1
                ins.then_inc(dve_link, 1)
                if n[0] == 1:
                    wait_apart(dve, (dve_link, s * NORM_LINKS + 1))
                else:
                    dve.wait_ge(dve_link, s * NORM_LINKS + n[0])

            def src(t):
                return rb[:, t, :] if inner else x[:, bass.ds(c * TPC + t, 1), :]

            for t in range(TPC):
                last = nc.vector.bn_stats(stats[:, t, :], src(t))
            link(last)
            for t in range(TPC):
                last = nc.vector.bn_aggr(mv[:, t, :], stats[:, t, :])
            link(last)
            link(nc.vector.tensor_scalar(var[:], mv[:, :, 1], EPS, None, ALU.add))
            link(nc.vector.tensor_scalar(nt[:].bitcast(i32), var[:].bitcast(i32), 1, None,
                                         ALU.logical_shift_right))
            link(nc.vector.tensor_scalar(rstd[:].bitcast(i32), nt[:].bitcast(i32), -1.0,
                                         float(RSQRT_GUESS), ALU.mult, ALU.add))
            for _ in range(3):
                link(nc.vector.tensor_tensor(nt[:], rstd[:], rstd[:], ALU.mult))
                link(nc.vector.scalar_tensor_tensor(nt[:], nt[:], -0.5, var[:], ALU.mult, ALU.mult))
                link(nc.vector.scalar_tensor_tensor(rstd[:], nt[:], 1.5, rstd[:], ALU.add, ALU.mult))
            assert n[0] == NORM_LINKS
            wait(dve, tr_ready, s)
            wait(dve, xb_ready, xb_made)
            for t in range(TPC):
                last = nc.vector.tensor_scalar(xn[:, t, :], src(t), mv[:, t, 0:1], rstd[:, t:t + 1],
                                               ALU.subtract, ALU.mult)
            last.then_inc(xn_ready, 1)

        def dve_low_input(dve, s, c):
            dve.wait_ge(xTh_done, s + 1)
            chunk = bass.ds(c * CHUNK, CHUNK)
            nc.vector.tensor_tensor(xT[:, 1, :, chunk], xTf[:], xT[:, 0, :, chunk].bitcast(f32),
                                    ALU.subtract).then_inc(xT_ready, 1)

        def dve_step(dve, p, at, prev):
            g, s, c, blk, par, kind = at

            def low(j):
                dve.wait_ge(round_done, HT * g + j + 1)
                nc.vector.tensor_tensor(hid[:, 1, j % 4, :], gel[:, j % 4, :],
                                        hid[:, 0, j % 4, :].bitcast(f32), ALU.subtract).then_inc(low_done, 1)

            for j in range(HT):
                if prev is not None:
                    if j == 0:
                        dve_take(dve, p, prev)
                    if prev[5] != "final":
                        if j == 2:
                            dve_norm(dve, prev[1], prev[2], prev[5] == "inner", xb_before(p, prev))
                        if j == 6:
                            dve_low_input(dve, prev[1], prev[2])
                low(j)

        def pool_xb(pool, s, c, blk, scaled):
            wait_apart(pool, (xn_ready, s + 1))
            tiles = bass.ds(c * TPC, TPC)

            def row(r):
                return rows[:, bass.ds(r, 1), :].broadcast_to([PART, TPC, DIM])

            if blk is None:
                nc.gpsimd.tensor_tensor(xb[:, tiles, :], xn[:], row(B2_1), ALU.add).then_inc(xb_ready, 1)
            else:
                nc.gpsimd.tensor_tensor(xb[:, tiles, :], xn[:], row(GAIN + blk), ALU.mult)\
                    .then_inc(xb_scaled, 1)
                wait_apart(pool, (xb_scaled, scaled + 1))
                nc.gpsimd.tensor_tensor(xb[:, tiles, :], xb[:, tiles, :], row(B2_1 + 1 + blk), ALU.add)\
                    .then_inc(xb_ready, 1)

        def pool_split(pool, n, q, par):
            if q == 0:
                wait_apart(pool, (w_loaded, 16 * (n + 1)),
                           (mm2_done, (n - 1) * (HT * CHUNKS)))
            half, cols = q // 2, slice(q % 2 * HIDDEN, (q % 2 + 1) * HIDDEN)
            nc.gpsimd.tensor_copy(w[par][:, 0, half, cols], wraw[:, half, cols]).then_inc(w_high, 1)
            pool.wait_ge(w_high, n * 4 + q + 1)
            nc.gpsimd.tensor_tensor(w[par][:, 1, half, cols], wraw[:, half, cols],
                                    w[par][:, 0, half, cols].bitcast(f32), ALU.subtract).then_inc(w_split, 1)

        def pool_post(pool, p, at):
            g, s, c, blk, par, kind = at
            if p.k == 1:
                pool_xb(pool, s, c, None, None)
            elif p.l1 and kind == "inner":
                pool_xb(pool, s, c, blk, CHUNKS * blk + c + (CHUNKS * (BLOCKS - 1) if p.k == 3 else 0))

        def pool_step(pool, p, at, prev):
            g, s, c, blk, par, kind = at
            if prev is not None:
                pool_post(pool, p, prev)
            if kind == "inner" or p.k == 1:
                if isinstance(c, int):
                    pool_split(pool, p.n0 + blk + 1, 0, 1 - par)
                    pool_split(pool, p.n0 + blk + 1, 1, 1 - par)
                    pool_split(pool, p.n0 + blk + 1, 2, 1 - par)
                    pool_split(pool, p.n0 + blk + 1, 3, 1 - par)

        def xb_before(p, at):
            g, s, c, blk, par, kind = at
            if p.k == 0:
                return 0
            if p.k == 1:
                return c
            if p.k == 2:
                return CHUNKS + CHUNKS * blk + c if kind == "inner" else CHUNKS * BLOCKS
            return CHUNKS * BLOCKS + CHUNKS + CHUNKS * blk + c

        S_PS, T_PS, AV_PS, MISC_PS = 0, 4, 6, 7

        def plan(kind):
            todo = []
            if kind == 1:
                todo += [("proj", "k", 0, 0), ("proj", "k", 0, 1), ("proj", "v", 0, 2), ("proj", "v", 0, 3),
                         ("vt", 0), ("vt", 1), ("proj", "q", 0, 4), ("proj", "q", 0, 5)]
            misc = 6
            todo += [("s", 0, qt) for qt in range(4)]
            if kind == 1:
                todo += [("proj", "q", 1, misc), ("proj", "q", 1, misc + 1)]
                misc += 2
            for h in range(GROUP):
                todo += [("s", h, 4), ("s", h, 5), ("pv", h, 0), ("s", h, 6), ("s", h, 7)]
                if kind == 1:
                    todo += [("wo", h, 0, misc), ("wo", h, 1, misc + 1)]
                    misc += 2
                if h + 1 < GROUP:
                    todo += [("s", h + 1, qt) for qt in range(4)]
                todo += [("pv", h, 1)]
                if kind == 1:
                    if h + 2 < GROUP:
                        todo += [("proj", "q", h + 2, misc), ("proj", "q", h + 2, misc + 1)]
                        misc += 2
                    todo += [("wo", h, 2, misc), ("wo", h, 3, misc + 1)]
                    misc += 2
            if kind == 0:
                todo += [("out", r) for r in range(4)]
            assert kind == 0 or misc == A1_MISC
            return todo

        def tiles_of(qc):
            return [(m + 4 * qc, m, max(0, m - 4 * qc)) for m in range(4 + 4 * qc)]

        def group_loop(e, kind, body):
            with e.Fori(0, BATCH) as b:
                with e.Fori(0, GROUPS // BATCH) as g:
                    i1 = b * (GROUPS // BATCH) + g
                    body(i1 + GROUPS * kind, i1, b, g)

        def a1_piece(part, which, h=0, k=0):
            at = {"k": 0, "v": 1, "q": 2 + h, "o": 6 + h}[which] * DIM
            if which == "o":
                return w_a1[:, part, at:at + DIM]
            return w_a1[:, part, at + k * HD1:at + (k + 1) * HD1]

        A1_PIECE = {"k": 0, "v": 1, "q": 2, "o": 6}

        def pe_att(pe, kind, i, i1, b, g):
            ql = q_sb if kind else q_st
            misc0 = A1_MISC * i1

            def scores(h, qt):
                u, width = GROUP * i + h, (qt + 1) * PART
                if not (h == 0 and qt < 2):
                    pe.wait_ge(exp_done, QT * u + qt - 1)
                if qt == 0:
                    if kind:
                        pe.wait_ge(misc_free, misc0 + {0: 6, 1: 8, 2: 12, 3: 18}[h])
                    else:
                        pe.wait_ge(qk_loaded[h % 2], 128 * (2 * i + h // 2 + 1))
                base = S_PS + 2 * (qt % 2)
                for bank in range((width + CHUNK - 1) // CHUNK):
                    n = min(CHUNK, width - bank * CHUNK)
                    dst = ps[:, base + bank, 0:n]
                    q, k = slice(qt * PART, (qt + 1) * PART), slice(bank * CHUNK, bank * CHUNK + n)
                    diagonal = bank == qt // 4
                    if kind:
                        for x3, (qp, kp) in enumerate(PARTS):
                            last = nc.tensor.matmul(dst, q_sb[:, h % 2, qp, q], k_sb[:, kp, k],
                                                    start=x3 == 0, stop=x3 == 2 and not diagonal)
                    else:
                        last = nc.tensor.matmul(dst, q_st[:, h % 2, q], k_st[:, h % 2, k],
                                                start=True, stop=not diagonal)
                    if diagonal:
                        last = nc.tensor.matmul(ps[:, base + bank, n - PART:n], ident_b[:], mask_b[:],
                                                start=False, stop=True)
                last.then_inc(s_ready, 1)

            def pv(h, qc):
                u = GROUP * i + h
                pe.wait_ge(p_ready, QT * u + 4 * qc + 4)
                p = p_hi if qc else p_lo

                def transpose(m, kt, q0):
                    if not (h == 0 and m < 2):
                        pe.wait_ge(pt_low, 12 * u + m - 1)
                    for qi in range(q0, TPC):
                        last = nc.tensor.transpose(ps[:, T_PS + m % 2, qi * PART:(qi + 1) * PART],
                                                   p[:, qi, kt * PART:(kt + 1) * PART], ident[:])
                    last.then_inc(pt_ready, 1)

                def product(m, kt, q0):
                    pe.wait_ge(pt_low, 12 * u + m + 1)
                    if kt == 0 and not (h == 0 and qc == 0):
                        pe.wait_ge(ctx_low, 2 * u + qc)
                    cols = slice(q0 * PART, CHUNK)
                    passes = ([(v_sb[:, vp, kt, :], pp) for vp, pp in PARTS] if kind
                              else [(v_st[:, kt, :], 1), (v_st[:, kt, :], 0)])
                    for n, (v, pp) in enumerate(passes):
                        last = nc.tensor.matmul(ps[:, AV_PS, cols], v, pT[:, pp, m % 2, cols],
                                                start=kt == 0 and n == 0,
                                                stop=kt == 3 + 4 * qc and n == len(passes) - 1)
                    last.then_inc(av_done, 1)

                if kind == 0 and h == 0 and qc == 0:
                    pe.wait_ge(v_loaded, 16 * (i + 1))
                tiles = tiles_of(qc)
                transpose(*tiles[0])
                for n, t in enumerate(tiles):
                    if n + 1 < len(tiles):
                        transpose(*tiles[n + 1])
                    product(*t)

            def project(which, h, n):
                pe.wait_ge(w1_split, 10 * i1 + A1_PIECE[which] + h + 1)
                if n:
                    pe.wait_ge(misc_free, misc0 + n)
                first = True
                for wp, xp in PARTS:
                    for k in range(KD):
                        last = nc.tensor.matmul(ps[:, MISC_PS, :], a1_piece(wp, which, h, k),
                                                xT[:, xp, k, bass.ds(b * SEQ + n % 2 * CHUNK, CHUNK)],
                                                start=first, stop=(wp, xp) == (0, 0) and k == KD - 1)
                        first = False
                last.then_inc(misc_ready, 1)

            def v_transpose(r):
                pe.wait_ge(misc_free, misc0 + 3 + r)
                for t in range(TPC):
                    last = nc.tensor.transpose(ps[:, T_PS + r, t * PART:(t + 1) * PART],
                                               xTf[:, r, t * PART:(t + 1) * PART], ident[:])
                last.then_inc(vt_ready, 1)

            def out_tiles(bank, t0, weight, done):
                for t in range(2):
                    for n, (cp, wp) in enumerate(PARTS):
                        last = nc.tensor.matmul(ps[:, bank, t * DIM:(t + 1) * DIM],
                                                ctxT[:, cp, (t0 + t) * PART:(t0 + t + 1) * PART], weight(wp),
                                                start=t == 0 and n == 0, stop=n == 2, skip_group_check=True)
                last.then_inc(done, 1)

            for op, *z in plan(kind):
                if op == "s":
                    scores(*z)
                elif op == "pv":
                    pv(*z)
                elif op == "proj":
                    project(*z)
                elif op == "vt":
                    v_transpose(*z)
                elif op == "wo":
                    h, r, n = z
                    pe.wait_ge(ctx_low, 2 * (GROUP * i + h) + r // 2 + 1)
                    pe.wait_ge(misc_free, misc0 + n)
                    pe.wait_ge(w1_split, 10 * i1 + 6 + h + 1)
                    out_tiles(MISC_PS, 2 * r, lambda wp: a1_piece(wp, "o", h), misc_ready)
                elif op == "out":
                    r, = z
                    if r == 0:
                        pe.wait_ge(ctx_low, 2 * GROUP * (i + 1))
                    if r >= 2:
                        pe.wait_ge(out_added, 4 * i + r - 1)
                    out_tiles((MISC_PS, AV_PS)[r % 2], 2 * r,
                              lambda wp: w_a0[:, wp, bass.ds(g * DIM + 5 * KD * DIM, DIM)], out_ready)
                    if r == 3:
                        pe.wait_ge(out_added, 4 * (i + 1))
            if kind:
                pe.wait_ge(misc_free, misc0 + A1_MISC)

        def act_att(act, kind, i, i1, b, g):
            misc0 = A1_MISC * i1
            for op, *z in plan(kind):
                if op == "s":
                    h, qt = z
                    u, width = GROUP * i + h, (qt + 1) * PART
                    act.wait_ge(max_ready, QT * u + qt + 1)
                    if h:
                        act.wait_ge(pt_ready, 12 * (u - 1) + (12 if qt >= 4 else 4))
                    base, p = S_PS + 2 * (qt % 2), p_hi if qt >= 4 else p_lo
                    nc.scalar.activation(p[:, qt % 4, 0:width],
                                         ps[:, base:base + 2, :].rearrange("p b n -> p (b n)")[:, 0:width],
                                         ACT.Exp, bias=negmax[:, qt:qt + 1],
                                         accum_out=rowsum[:, qt:qt + 1]).then_inc(exp_done, 1)
                elif op == "pv":
                    h, qc = z
                    u = GROUP * i + h
                    for m, kt, q0 in tiles_of(qc):
                        act.wait_ge(pt_ready, 12 * u + m + 1)
                        if not (h == 0 and m < 2):
                            act.wait_ge(av_done, 12 * u + m - 1)
                        nc.scalar.activation(pT[:, 0, m % 2, q0 * PART:], ps[:, T_PS + m % 2, q0 * PART:],
                                             ACT.Copy).then_inc(pt_high, 1)
                    act.wait_ge(av_done, 12 * u + 4 + 8 * qc)
                    if kind:
                        if h:
                            act.wait_ge(misc_ready, misc0 + WO_DONE[h - 1][qc])
                        rows_ = slice(0, PART)
                    else:
                        rows_ = slice(32 * h, 32 * h + 32)
                    nc.scalar.activation(ctxT[rows_, 0, qc * CHUNK:(qc + 1) * CHUNK], ps[rows_, AV_PS, :],
                                         ACT.Copy).then_inc(ctx_high, 1)
                elif op == "proj" and z[0] != "v":
                    which, h, n = z
                    act.wait_ge(misc_ready, misc0 + n + 1)
                    dst = (k_sb[:, 0, :] if which == "k" else q_sb[:, h % 2, 0, :])
                    nc.scalar.activation(dst[:, n % 2 * CHUNK:(n % 2 + 1) * CHUNK], ps[:, MISC_PS, :],
                                         ACT.Copy).then_inc(misc_high, 1)
                elif op == "vt":
                    r, = z
                    act.wait_ge(vt_ready, 2 * i1 + r + 1)
                    nc.scalar.activation(v_sb[:, 0, 4 * r:4 * r + 4, :].rearrange("p t n -> p (t n)"),
                                         ps[:, T_PS + r, :], ACT.Copy).then_inc(vt_high, 1)

        def dve_att(dve, kind, i, i1, b, g):
            misc0 = A1_MISC * i1
            pending, highs = [], [0]

            def normalise():
                h, qt = pending.pop()
                u, width = GROUP * i + h, (qt + 1) * PART
                dve.wait_ge(exp_done, QT * u + qt + 1)
                nc.vector.reciprocal(rowinv[:, qt:qt + 1], rowsum[:, qt:qt + 1]).then_inc(inv_ready, 1)
                dve.wait_ge(inv_ready, QT * u + qt + 1)
                p = (p_hi if qt >= 4 else p_lo)[:, qt % 4, 0:width]
                nc.vector.tensor_scalar(p, p, rowinv[:, qt:qt + 1], None, ALU.mult).then_inc(p_ready, 1)

            def add_out(bank, t0, ready, ready_at, done):
                dve.wait_ge(ready, ready_at)
                dst = x[:, bass.ds(b * QT + t0, 2), :]
                nc.vector.tensor_tensor(dst, ps[:, bank, :].rearrange("p (t e) -> p t e", t=2), dst,
                                        ALU.add).then_inc(done, 1)

            for op, *z in plan(kind):
                if op == "s":
                    h, qt = z
                    u, width = GROUP * i + h, (qt + 1) * PART
                    dve.wait_ge(s_ready, QT * u + qt + 1)
                    base = S_PS + 2 * (qt % 2)
                    nc.vector.tensor_reduce(
                        negmax[:, qt:qt + 1],
                        ps[:, base:base + 2, :].rearrange("p b n -> p (b n)")[:, 0:width],
                        AX.X, ALU.max, negate=True).then_inc(max_ready, 1)
                    if pending:
                        normalise()
                    pending.append((h, qt))
                elif op == "pv":
                    h, qc = z
                    u = GROUP * i + h
                    for n, (m, kt, q0) in enumerate(tiles_of(qc)):
                        if pending and (n == 1 or pending[-1] == (h, 7)):
                            normalise()
                        dve.wait_ge(pt_high, 12 * u + m + 1)
                        nc.vector.tensor_tensor(pT[:, 1, m % 2, q0 * PART:], ps[:, T_PS + m % 2, q0 * PART:],
                                                pT[:, 0, m % 2, q0 * PART:].bitcast(f32),
                                                ALU.subtract).then_inc(pt_low, 1)
                    dve.wait_ge(ctx_high, 2 * u + qc + 1)
                    rows_ = slice(0, PART) if kind else slice(32 * h, 32 * h + 32)
                    cols = slice(qc * CHUNK, (qc + 1) * CHUNK)
                    nc.vector.tensor_tensor(ctxT[rows_, 1, cols], ps[rows_, AV_PS, :],
                                            ctxT[rows_, 0, cols].bitcast(f32), ALU.subtract)\
                        .then_inc(ctx_low, 1)
                elif op == "proj":
                    which, h, n = z
                    half = slice(n % 2 * CHUNK, (n % 2 + 1) * CHUNK)
                    if which == "v":
                        dve.wait_ge(misc_ready, misc0 + n + 1)
                        nc.vector.tensor_copy(xTf[:, n % 2, :], ps[:, MISC_PS, :]).then_inc(misc_free, 1)
                    else:
                        highs[0] += 1
                        dve.wait_ge(misc_high, 10 * i1 + highs[0])
                        high, low = ((k_sb[:, 0, half], k_sb[:, 1, half]) if which == "k" else
                                     (q_sb[:, h % 2, 0, half], q_sb[:, h % 2, 1, half]))
                        nc.vector.tensor_tensor(low, ps[:, MISC_PS, :], high.bitcast(f32), ALU.subtract)\
                            .then_inc(misc_free, 1)
                elif op == "vt":
                    r, = z
                    dve.wait_ge(vt_high, 2 * i1 + r + 1)
                    at = [v_sb[:, part, 4 * r:4 * r + 4, :].rearrange("p t n -> p (t n)") for part in (0, 1)]
                    nc.vector.tensor_tensor(at[1], ps[:, T_PS + r, :], at[0].bitcast(f32), ALU.subtract)\
                        .then_inc(vt_low, 1)
                elif op == "wo":
                    h, r, n = z
                    add_out(MISC_PS, 2 * r, misc_ready, misc0 + n + 1, misc_free)
                elif op == "out":
                    r, = z
                    add_out((MISC_PS, AV_PS)[r % 2], 2 * r, out_ready, 4 * i + r + 1, out_added)

        WO_DONE = {}
        for op, *z in plan(1):
            if op == "wo":
                WO_DONE.setdefault(z[0], {})[z[1] // 2] = z[2] + 1

        def last_use(piece):
            n = 0
            for op, *z in plan(1):
                if op == "proj" and A1_PIECE[z[0]] + z[1] == piece or op == "wo" and 6 + z[0] == piece:
                    n = z[-1] + 1
            return n

        def pool_split_a1(pool, i, first):
            wait_apart(pool, (w1_loaded, 16 * (i + 1)))
            for piece in range(10):
                cols = slice(piece * DIM, (piece + 1) * DIM)
                if not first:
                    wait_apart(pool, (misc_ready, A1_MISC * (i - 1) + last_use(piece)))
                nc.gpsimd.tensor_copy(w_a1[:, 0, cols], xb[:, piece, :]).then_inc(w1_high, 1)
                pool.wait_ge(w1_high, 10 * i + piece + 1)
                nc.gpsimd.tensor_tensor(w_a1[:, 1, cols], xb[:, piece, :], w_a1[:, 0, cols].bitcast(f32),
                                        ALU.subtract).then_inc(w1_split, 1)

        PIECES = [(qk, half) for qk in range(2) for half in range(KD)]
        V_W = 4 * KD * DIM

        def a0_raw(piece):
            bounds = [0, 2 * KD * DIM, 4 * KD * DIM, A0_W]
            return slice(bounds[piece], bounds[piece + 1])

        xb_flat = xb[:, :, :].rearrange("p t e -> p (t e)")

        def rope_pieces(e, body):
            with e.Fori(0, BATCH) as b:
                for m in range(2 * len(PIECES)):
                    sc, (qk, half) = m // len(PIECES), PIECES[m % len(PIECES)]
                    body(b * (2 * len(PIECES)) + m, b * SEQ + sc * CHUNK, sc * CHUNK, qk, half, m % 2, m, b * len(PIECES) + m // 2)

        def pe_project_a0(pe):
            pe.wait_ge(xT_ready, S_ATT[0])

            def piece(n, token, seq, qk, half, slot, m, half_n):
                if m >= 2:
                    pe.wait_ge(rope_taken, n - 1)
                for swap in range(2):
                    pe.wait_ge(a_low, qk + 1)
                    first = True
                    for wp, xp in PARTS:
                        for k in range(KD):
                            at = ((2 * qk + swap) * KD + k) * DIM + half * PART
                            last = nc.tensor.matmul(ps[:, 2 * slot + swap, :], w_a0[:, wp, at:at + PART],
                                                    xT[:, xp, k, bass.ds(token, CHUNK)], start=first,
                                                    stop=(wp, xp) == (0, 0) and k == KD - 1)
                            first = False
                last.then_inc(proj_ready, 1)
                if m == 2 * len(PIECES) - 1:
                    pe.wait_ge(rope_taken, n + 1)

            rope_pieces(pe, piece)
            pe.wait_ge(a_low, 3)
            for t in range(TILES):
                wait(pe, v_low, t - 1)
                first = True
                for wp, xp in PARTS:
                    for k in range(KD):
                        last = nc.tensor.matmul(ps[:, 4 + t % 2, 0:DIM],
                                                xT[:, xp, k, t * PART:(t + 1) * PART],
                                                w_a0[:, wp, V_W + k * DIM:V_W + (k + 1) * DIM], start=first,
                                                stop=(wp, xp) == (0, 0) and k == KD - 1)
                        first = False
                last.then_inc(v_ready, 1)
            pe.wait_ge(v_low, TILES)

        def act_project_a0(act):
            act.wait_ge(a_loaded, 16)
            act.wait_ge(xT_ready, S_ATT[0])
            for piece in range(3):
                nc.scalar.activation(w_a0[:, 0, a0_raw(piece)], xb_flat[:, a0_raw(piece)], ACT.Copy)\
                    .then_inc(a_high, 1)

            def piece(n, token, seq, qk, half, slot, m, half_n):
                act.wait_ge(rope_sum, n + 1)
                if m >= 2:
                    act.wait_ge(rope_stored[slot], 16 * half_n)
                nc.scalar.activation(rope_hl[:, 0, slot, :], rope[:, 2, slot, :], ACT.Copy)\
                    .then_inc(rope_high, 1)
                if m == 2 * len(PIECES) - 1:
                    for stored in rope_stored:
                        act.wait_ge(stored, 16 * (half_n + 1))

            rope_pieces(act, piece)
            for t in range(TILES):
                act.wait_ge(v_ready, t + 1)
                wait(act, v_stored[t % 2], 16 * (t // 2))
                nc.scalar.activation(v_hl[:, t % 2, :, 0, :],
                                     ps[:, 4 + t % 2, 0:DIM].rearrange("p (h d) -> p h d", h=HEADS),
                                     ACT.Copy).then_inc(v_high, 1)

        def dve_project_a0(dve):
            for piece in range(3):
                dve.wait_ge(a_high, piece + 1)
                nc.vector.tensor_tensor(w_a0[:, 1, a0_raw(piece)], xb_flat[:, a0_raw(piece)],
                                        w_a0[:, 0, a0_raw(piece)].bitcast(f32), ALU.subtract)\
                    .then_inc(a_low, 1)
            dve.wait_ge(a_low, 3)
            dve.wait_ge(att_tab, 16)

            def piece(n, token, seq, qk, half, slot, m, half_n):
                dve.wait_ge(proj_ready, n + 1)
                for term in range(2):
                    nc.vector.tensor_tensor(rope[:, term, slot, :], ps[:, 2 * slot + term, :],
                                            rot[:, 2 * qk + term, seq:seq + CHUNK], ALU.mult)\
                        .then_inc((rope_term, rope_taken)[term], 1)
                dve.wait_ge(rope_taken, n + 1)
                nc.vector.tensor_tensor(rope[:, 2, slot, :], rope[:, 0, slot, :], rope[:, 1, slot, :],
                                        ALU.add).then_inc(rope_sum, 1)
                dve.wait_ge(rope_high, n + 1)
                nc.vector.tensor_tensor(rope_hl[:, 1, slot, :], rope[:, 2, slot, :],
                                        rope_hl[:, 0, slot, :].bitcast(f32), ALU.subtract)\
                    .then_inc(rope_low, 1)

            rope_pieces(dve, piece)
            for t in range(TILES):
                dve.wait_ge(v_high, t + 1)
                nc.vector.tensor_tensor(v_hl[:, t % 2, :, 1, :],
                                        ps[:, 4 + t % 2, 0:DIM].rearrange("p (h d) -> p h d", h=HEADS),
                                        v_hl[:, t % 2, :, 0, :].bitcast(f32), ALU.subtract)\
                    .then_inc(v_low, 1)

        def sp_project_a0(sp):
            sp.wait_ge(xT_ready, S_ATT[0])
            sp.dma_start(xb_flat[:, 0:A0_W], a["w_a0"]).then_inc(a_loaded, 16)
            sp.dma_start(rot[:], a["rot"]).then_inc(att_tab, 16)

            def piece(n, token, seq, qk, half, slot, m, half_n):
                wait_apart(sp, (rope_low, n + 1))
                sp.dma_start(qk_dram[qk, half * PART:(half + 1) * PART, :, bass.ds(token, CHUNK)],
                             rope_hl[:, :, slot, :].bitcast(f32)).then_inc(rope_stored[slot], 16)

            rope_pieces(sp, piece)
            for t in range(TILES):
                sp.wait_ge(v_low, t + 1)
                sp.dma_start(v_dram[t, :, :],
                             v_hl[:, t % 2, :, :, :].rearrange("p h a d -> p (h a d)").bitcast(f32))\
                    .then_inc(v_stored[t % 2], 16)
            for stored in rope_stored:
                sp.wait_ge(stored, 16 * 2 * len(PIECES))
            for stored in v_stored:
                sp.wait_ge(stored, 16 * TILES // 2)

            def group(i, i1, b, g):
                for h in range(GROUP):
                    u = GROUP * i + h
                    if h >= 2:
                        wait_apart(sp, (s_ready, QT * (u - 1)))
                    for row, (qp, kp) in enumerate(((0, 0), (1, 0), (0, 1), (1, 1))):
                        for dst, qk, part in ((q_st, 0, qp), (k_st, 1, kp)):
                            sp.dma_start(dst[row * HD0:(row + 1) * HD0, h % 2, :].bitcast(f32),
                                         qk_dram[qk, bass.ds((GROUP * g + h) * HD0, HD0), part,
                                                 bass.ds(b * SEQ, SEQ)]).then_inc(qk_loaded[h % 2], 16)
                    if h == 0:
                        sp.dma_start(v_st[:].bitcast(f32), v_dram[bass.ds(b * QT, QT), :, bass.ds(g * PART, PART)]
                                     .rearrange("t p n -> p t n")).then_inc(v_loaded, 16)
                wait_apart(sp, (av_done, 12 * GROUP * (i + 1)))

            group_loop(sp, 0, group)

        def attention(e, kind, body):
            group_loop(e, kind, lambda i, i1, b, g: body(e, kind, i, i1, b, g))

        ATT_END = {0: (out_added, 4 * GROUPS), 1: (misc_free, A1_MISC * GROUPS)}
        S_ATT = {0: CHUNKS * 2, 1: CHUNKS * (2 + 1 + 1 + BLOCKS)}
        ATT_BEFORE = {1: 0, 3: 1}

        def x_ready(e, k):
            if k == 0:
                e.wait_ge(in_loaded, 16 * N_IN)
                e.wait_ge(tab_ready, 1)
            elif ATT_BEFORE[k] in ATTS:
                e.wait_ge(*ATT_END[ATT_BEFORE[k]])

        def pre_posts(e, k, body):
            p = phase(k)
            if p.pre:
                body(p, p.s0 - CHUNKS, 0)
                with e.Fori(1, CHUNKS) as c:
                    body(p, p.s0 - CHUNKS + c, c)

        N_IN = 9

        block = ctx.enter_context(nc.Block())

        @block.sync
        def _(sp):
            for t in range(CHUNKS):
                tiles = slice(t * TPC, (t + 1) * TPC)
                sp.dma_start(x[:, tiles, :], a["x"].rearrange("(t p) e -> p t e", p=PART)[:, tiles, :])\
                    .then_inc(in_loaded, 16)
            sp.dma_start(ident[:], a["ident"]).then_inc(in_loaded, 16)
            sp.dma_start(b1[:], a["b1"]).then_inc(in_loaded, 16)
            sp.dma_start(gT[:, KD:], a["gT"]).then_inc(in_loaded, 16)
            sp.dma_start(bT[:, KD:], a["bT"]).then_inc(in_loaded, 16)
            sp.dma_start(rows[:], a["rows"].partition_broadcast(PART)).then_inc(in_loaded, 16)
            sp.dma_start(lnb[:], a["lnb"].partition_broadcast(PART)).then_inc(lnb_loaded, 16)
            sp.dma_start(rb[:, 0, 0:PART], a["mask"]).then_inc(lnb_loaded, 16)

            def load(n, source):
                wait_apart(sp, (w_split, 4 * n))
                sp.dma_start(wraw[:], a["wffn"][bass.ds(source, 1), :, :].rearrange(
                    "o p (h n) -> p (o h) n", h=2)).then_inc(w_loaded, 16)

            for k in range(LASTK + 1):
                p = phase(k)
                if k == 1 and 0 in ATTS:
                    sp_project_a0(sp)
                if k == 3 and 1 in ATTS:
                    sp.wait_ge(xT_ready, S_ATT[1])
                    sp.dma_start(xb[:, 0:10, :], a["w_a1"][0, :, :].rearrange("p (t e) -> p t e", e=DIM))\
                        .then_inc(w1_loaded, 16)
                    with sp.Fori(1, GROUPS) as i:
                        wait_apart(sp, (w1_split, 10 * i))
                        sp.dma_start(xb[:, 0:10, :], a["w_a1"][bass.ds(i, 1), :, :].rearrange(
                            "o p (t e) -> p (o t) e", e=DIM)).then_inc(w1_loaded, 16)
                if p.pre:
                    x_ready(sp, k)
                if k != 2:
                    load(p.n0, p.tab)
                if k == 1:
                    load(p.n0 + 1, 1)
                if p.l1:
                    with sp.Fori(1, p.blocks) as blk:
                        load(p.n0 + blk, p.tab + blk)
            if FINAL:
                for c in range(CHUNKS):
                    sp.wait_ge(x_updated, 4 * CHUNKS + c + 1)
                    sp.dma_start(a["out"].rearrange("(t p) e -> p t e", p=PART)[:, c * TPC:(c + 1) * TPC, :],
                                 x[:, c * TPC:(c + 1) * TPC, :]).then_inc(out_stored, 16)
            else:
                sp.wait_ge(x_updated, CHUNKS * (LASTK + 1))
                for c in range(CHUNKS):
                    sp.dma_start(a["out"].rearrange("(t p) e -> p t e", p=PART)[:, c * TPC:(c + 1) * TPC, :],
                                 x[:, c * TPC:(c + 1) * TPC, :]).then_inc(out_stored, 16)
            sp.wait_ge(out_stored, 16 * CHUNKS)

        @block.gpsimd
        def _(pool):
            nc.gpsimd.memset(gT[:, 0:KD], 1.0)
            nc.gpsimd.memset(bT[:, 0:KD], 0.0).then_inc(tab_ready, 1)
            pool.wait_ge(in_loaded, 16 * N_IN)
            pool.wait_ge(lnb_loaded, 32)
            nc.gpsimd.tensor_copy(ident_b[:], ident[:]).then_inc(ident_ready, 1)
            nc.gpsimd.tensor_copy(mask_b[:], rb[:, 0, 0:PART]).then_inc(ident_ready, 1)
            nc.gpsimd.tensor_tensor(rows[:, B2_1 + 1:B2_1 + BLOCKS, :], rows[:, B2_1 + 1:B2_1 + BLOCKS, :],
                                    lnb[:], ALU.add).then_inc(rows_ready, 1)
            pool.wait_ge(rows_ready, 1)
            for k in range(LASTK + 1):
                p = phase(k)
                if k == 3 and 1 in ATTS:
                    pool_split_a1(pool, 0, True)
                    with pool.Fori(1, GROUPS) as i:
                        pool_split_a1(pool, i, False)
                if p.pre:
                    x_ready(pool, k)
                if k != 2:
                    for q in range(4):
                        pool_split(pool, p.n0, q, p.n0 % 2)
                if k == 3:
                    pre_posts(pool, k, lambda p, s, c: pool_xb(pool, s, c, None, None))
                walk(p, pool, lambda at, prev: pool_step(pool, p, at, prev))
                pool_post(pool, p, tail(p))

        @block.scalar
        def _(act):
            act.wait_ge(in_loaded, 16 * N_IN)
            act.wait_ge(tab_ready, 1)
            for k in range(LASTK + 1):
                p = phase(k)
                if k == 1 and 0 in ATTS:
                    act_project_a0(act)
                    attention(act, 0, act_att)
                if k == 3 and 1 in ATTS:
                    act.wait_ge(xT_ready, S_ATT[1])
                    attention(act, 1, act_att)
                pre_posts(act, k, lambda p, s, c: act_affine(act, s, c, 0))
                walk(p, act, lambda at, prev: act_step(act, p, at, prev))
                if p.last != "final":
                    act_affine(act, tail(p)[1], CHUNKS - 1, 0)

        @block.vector
        def _(dve):
            dve.wait_ge(ident_ready, 2)
            for k in range(LASTK + 1):
                p = phase(k)

                def pre(p, s, c):
                    if p.k == 3:
                        tiles = bass.ds(c * TPC, TPC)
                        nc.vector.tensor_tensor(x[:, tiles, :], x[:, tiles, :], rows[:, BO:BO + 1, :]
                                                .broadcast_to([PART, TPC, DIM]), ALU.add).then_inc(x_updated, 1)
                        wait_apart(dve, (x_updated, 3 * CHUNKS + c + 1))
                    dve_norm(dve, s, c, False, CHUNKS * BLOCKS + c if p.k == 3 else 0)
                    dve_low_input(dve, s, c)

                if k == 1 and 0 in ATTS:
                    dve_project_a0(dve)
                    attention(dve, 0, dve_att)
                if k == 3 and 1 in ATTS:
                    attention(dve, 1, dve_att)
                if p.pre:
                    x_ready(dve, k)
                pre_posts(dve, k, pre)
                walk(p, dve, lambda at, prev: dve_step(dve, p, at, prev))
                dve_take(dve, p, tail(p))
                if p.last != "final":
                    dve_norm(dve, tail(p)[1], CHUNKS - 1, False, xb_before(p, tail(p)))
                    dve_low_input(dve, tail(p)[1], CHUNKS - 1)

        @block.tensor
        def _(pe):
            pe.wait_ge(in_loaded, 16 * N_IN)
            for k in range(LASTK + 1):
                p = phase(k)
                if k == 1 and 0 in ATTS:
                    pe.wait_ge(ident_ready, 2)
                    pe_project_a0(pe)
                    attention(pe, 0, pe_att)
                if k == 3 and 1 in ATTS:
                    pe.wait_ge(xT_ready, S_ATT[1])
                    attention(pe, 1, pe_att)
                pre_posts(pe, k, lambda p, s, c: pe_transpose_chunk(pe, s))
                walk(p, pe, lambda at, prev: pe_step(pe, p, at, prev))
                if p.last != "final":
                    pe_transpose_chunk(pe, tail(p)[1])


def rotation():
    f = np.float32
    inverse = (f(1) / np.power(f(ROPE_BASE), np.arange(0, HD0, 2, dtype=f) / f(HD0))).astype(f)
    angles = np.outer(inverse, np.arange(SEQ, dtype=f)).astype(f)
    cos = np.tile(np.cos(angles), (2, 1))
    sin = np.concatenate([-np.sin(angles), np.sin(angles)])
    one = np.stack([np.tile(v, (PART // HD0, 1)) for v in (cos, sin)], axis=1)
    return np.concatenate([one * f(HD0 ** -0.5), one], axis=1).astype(f)


def layout(d):
    f = np.float32

    def columns(v):
        return np.ascontiguousarray(v.reshape(-1, PART).T)

    def ffn(w1, w2):
        one = w1.T.reshape(KD, PART, HIDDEN).transpose(1, 0, 2).reshape(PART, -1)
        two = w2.T.reshape(HT, PART, DIM).transpose(1, 0, 2).reshape(PART, -1)
        return np.concatenate([one, two], axis=1)

    def heads(w, swap=False):
        if swap:
            w = w.reshape(HEADS, 2, HD0 // 2, DIM)[:, ::-1].reshape(DIM, DIM)
        return w.T.reshape(KD, PART, DIM).transpose(1, 0, 2).reshape(PART, -1)

    wq, wk, wv, wo = (d[f"L0_attn_{n}"] for n in ("Wq", "Wk", "Wv", "Wo"))
    stack = wo.T.reshape(GROUP, GROUP, 1, HD0, DIM).repeat(2, axis=2).reshape(GROUP, PART, DIM)
    w_a0 = np.concatenate([heads(wq), heads(wq, True), heads(wk), heads(wk, True), heads(wv),
                           stack.transpose(1, 0, 2).reshape(PART, -1)], axis=1)

    def columns_of(w):
        return w.T.reshape(KD, PART, HD1).transpose(1, 0, 2).reshape(PART, -1)

    wq1, wk1, wv1, wo1 = (d[f"L1_attn_{n}"] for n in ("Wq", "Wk", "Wv", "Wo"))
    groups = []
    for n in range(KV1):
        rows = slice(n * HD1, (n + 1) * HD1)
        mine = [slice((GROUP * n + h) * HD1, (GROUP * n + h + 1) * HD1) for h in range(GROUP)]
        groups.append(np.concatenate([columns_of(wk1[rows]), columns_of(wv1[rows])]
                                     + [columns_of(wq1[r]) for r in mine] + [wo1[:, r].T for r in mine], axis=1))
    w_a1 = np.stack(groups * BATCH)

    return {
        "w_a0": w_a0, "w_a1": w_a1, "rot": rotation(), "mask": np.triu(np.full((PART, PART), MASKED, f), 1),
        "x": np.ascontiguousarray(d["L0_attn_hidden_states"].reshape(TOKENS, DIM)),
        "ident": np.eye(PART, dtype=f),
        "b1": columns(np.concatenate([d["L0_ffn_proj1_bias"][None], d["L1_ffn_B1"]])),
        "gT": columns(d["L1_ffn_LN_G"]), "bT": columns(d["L1_ffn_LN_B"]),
        "rows": np.concatenate([d["L0_ffn_proj2_bias"][None], d["L1_attn_bo"][None], d["L1_ffn_B2"],
                                d["L1_ffn_LN_G"]]),
        "lnb": np.ascontiguousarray(d["L1_ffn_LN_B"]),
        "wffn": np.stack([ffn(d["L0_ffn_proj1"], d["L0_ffn_proj2"])]
                         + [ffn(d["L1_ffn_W1"][i], d["L1_ffn_W2"][i]) for i in range(BLOCKS)]),
    }


def kernel(**inputs):
    import concourse.bacc as bacc
    from concourse.bass_utils import run_bass_kernel_spmd

    arrays = {n: v for n, v in layout({k: np.asarray(v) for k, v in inputs.items()}).items()}
    nc = bacc.Bacc("TRN2", target_bir_lowering=False, num_devices=1)
    aps = {n: nc.dram_tensor(f"in_{n}", v.shape, mybir.dt.from_np(v.dtype), kind="ExternalInput").ap()
           for n, v in arrays.items()}
    aps["out"] = nc.dram_tensor("out", (TOKENS, DIM), mybir.dt.float32, kind="ExternalOutput").ap()
    build(nc, aps)
    r = run_bass_kernel_spmd(nc, [{f"in_{n}": v for n, v in arrays.items()}], core_ids=[0])
    return r.results[0]["out"].reshape(BATCH, SEQ, DIM)
```

```python
from contextlib import ExitStack

import concourse.bass as bass
import numpy as np
from concourse import mybir
from concourse.alu_op_type import AluOpType as ALU

PART = 128
BATCH, SEQ, DIM = 2, 1024, 256
TOKENS = BATCH * SEQ
HIDDEN = 1024
BLOCKS = 6
CHUNK = 512
CHUNKS = TOKENS // CHUNK
TILES = TOKENS // PART
TPC = CHUNK // PART
KD = DIM // PART
HT = HIDDEN // PART
EPS = 1e-5
HEADS = 16
HD0 = DIM // HEADS
HD1 = 128
KV1 = 4
GROUP = 4
GROUPS = BATCH * HEADS // GROUP
QT = SEQ // PART
ROPE_BASE = 10000.0
MASKED = -1e30
RSQRT_GUESS = 0x5F3759DF
A0_W = 5 * KD * DIM + GROUP * DIM
A1_W = 10 * DIM
A1_MISC = 4 + GROUP * 6
FFN_BLOCKS = (1, 1, BLOCKS, BLOCKS)
PT_SLOTS = 4
LAG = 2
PARTS = ((1, 0), (0, 1), (0, 0))


PRE = (0, 1, 3)


def build(nc, a, LASTK=3, FINAL=True, ATTS=(0, 1)):
    f32, f32r, i32, bf16 = mybir.dt.float32, mybir.dt.float32r, mybir.dt.int32, mybir.dt.bfloat16
    ACT = mybir.ActivationFunctionType
    AX = mybir.AxisListType
    ctx = ExitStack()
    with ctx:
        def sb(name, shape, dt=f32, stack=ctx):
            return stack.enter_context(nc.sbuf_tensor(name, shape, dt))

        def sem(name):
            return ctx.enter_context(nc.semaphore(name))

        x = sb("x", [PART, TILES, DIM])
        xT = sb("xT", [PART, 2, KD, TOKENS], f32r)
        xb = sb("xb", [PART, TILES, DIM])
        rb = sb("rb", [PART, TPC, DIM])
        xn = sb("xn", [PART, TPC, DIM])
        xTf = sb("xTf", [PART, KD, CHUNK])
        rows = sb("rows", [PART, 1 + 2 * BLOCKS, DIM])
        B2_0, BO, B2_1, GAIN = 0, 1, 2, 2 + BLOCKS
        lnb = sb("lnb", [PART, BLOCKS - 1, DIM])
        b1 = sb("b1", [PART, (1 + BLOCKS) * HT])
        gT = sb("gT", [PART, BLOCKS * KD])
        bT = sb("bT", [PART, BLOCKS * KD])
        ident = sb("ident", [PART, PART])
        stats = sb("stats", [PART, TPC, 6])
        mv = sb("mv", [PART, TPC, 2])
        var = sb("var", [PART, TPC])
        rstd = sb("rstd", [PART, TPC])
        nt = sb("nt", [PART, TPC])
        negmax = sb("negmax", [PART, QT])
        rowsum = sb("rowsum", [PART, 2, QT])
        rowinv = sb("rowinv", [PART, 2, QT])
        ident_b = sb("ident_b", [PART, PART], bf16)
        mask_b = sb("mask_b", [PART, PART], bf16)

        ffn = ExitStack()
        wraw = sb("wraw", [PART, 2, KD * HIDDEN], f32, ffn)
        w = [sb(f"w{p}", [PART, 2, 2, KD * HIDDEN], f32r, ffn) for p in range(2)]
        gel = sb("gel", [PART, 4, CHUNK], f32, ffn)
        hid = sb("hid", [PART, 2, 4, CHUNK], f32r, ffn)
        ffn.close()

        att = ExitStack()
        p_lo = sb("p_lo", [PART, TPC, SEQ // 2], f32, att)
        p_hi = sb("p_hi", [PART, TPC, SEQ], f32, att)
        pT = sb("pT", [PART, 2, PT_SLOTS, CHUNK], f32r, att)
        ctxT = sb("ctxT", [PART, 2, SEQ], f32r, att)
        q_sb = sb("q_sb", [PART, 2, 2, SEQ], f32r, att)
        k_sb = sb("k_sb", [PART, 2, SEQ], f32r, att)
        v_sb = sb("v_sb", [PART, 2, QT, HD1], f32r, att)
        w_a1 = sb("w_a1", [PART, 2, A1_W], f32r, att)
        att.close()
        att = ExitStack()
        for name, shape in (("p_lo0", [PART, TPC, SEQ // 2]), ("p_hi0", [PART, TPC, SEQ])):
            sb(name, shape, f32, att)
        sb("pT0", [PART, 2, PT_SLOTS, CHUNK], f32r, att)
        sb("ctxT0", [PART, 2, SEQ], f32r, att)
        q_st = sb("q_st", [64, 2, SEQ], f32r, att)
        k_st = sb("k_st", [64, 2, SEQ], f32r, att)
        v_st = sb("v_st", [PART, QT, PART], f32r, att)
        w_a0 = sb("w_a0", [PART, 2, A0_W], f32r, att)
        att.close()
        att = ExitStack()
        rot = sb("rot", [PART, 4, SEQ], f32, att)
        rope = sb("rope", [PART, 3, 2, CHUNK], f32, att)
        rope_hl = sb("rope_hl", [PART, 2, 2, CHUNK], f32r, att)
        v_hl = sb("v_hl", [PART, 2, HEADS, 2, HD0], f32r, att)
        att.close()

        qk_dram = nc.dram_tensor("qk_dram", (2, DIM, 2, TOKENS), f32, kind="Internal").ap()
        v_dram = nc.dram_tensor("v_dram", (TILES, PART, 2 * DIM), f32, kind="Internal").ap()
        ps = ctx.enter_context(nc.psum_tensor("ps", [PART, 8, CHUNK], f32))
        HPS, YPS, TPS = 0, 4, 6
        y_ps = ps[:, YPS:YPS + 2, :].rearrange("p b (t e) -> p (b t) e", e=DIM)

        in_loaded = sem("in_loaded")
        lnb_loaded = sem("lnb_loaded")
        tab_ready = sem("tab_ready")
        rows_ready = sem("rows_ready")
        w_loaded = sem("w_loaded")
        w_high = sem("w_high")
        w_split = sem("w_split")
        hid_ready = sem("hid_ready")
        gelu_done = sem("gelu_done")
        round_done = sem("round_done")
        low_done = sem("low_done")
        mm2_done = sem("mm2_done")
        y_free = sem("y_free")
        x_updated = sem("x_updated")
        xn_ready = sem("xn_ready")
        tr_ready = sem("tr_ready")
        aff_done = sem("aff_done")
        xTh_done = sem("xTh_done")
        xT_ready = sem("xT_ready")
        xb_scaled = sem("xb_scaled")
        xb_ready = sem("xb_ready")
        dve_link = sem("dve_link")
        out_stored = sem("out_stored")
        att_tab = sem("att_tab")
        ident_ready = sem("ident_ready")
        a_loaded = sem("a_loaded")
        a_high = sem("a_high")
        a_low = sem("a_low")
        proj_ready = sem("proj_ready")
        rope_term = sem("rope_term")
        rope_taken = sem("rope_taken")
        rope_sum = sem("rope_sum")
        rope_high = sem("rope_high")
        rope_low = sem("rope_low")
        v_ready = sem("v_ready")
        v_high = sem("v_high")
        v_low = sem("v_low")
        v_loaded = sem("v_loaded")
        s_ready = sem("s_ready")
        max_ready = sem("max_ready")
        exp_done = sem("exp_done")
        inv_ready = sem("inv_ready")
        p_by_act = sem("p_by_act")
        p_by_dve = sem("p_by_dve")
        pt_ready = sem("pt_ready")
        pt_high = sem("pt_high")
        pt_low = sem("pt_low")
        av_done = sem("av_done")
        ctx_high = sem("ctx_high")
        ctx_low = sem("ctx_low")
        out_ready = sem("out_ready")
        out_added = sem("out_added")
        misc_ready = sem("misc_ready")
        misc_high = sem("misc_high")
        misc_free = sem("misc_free")
        vt_ready = sem("vt_ready")
        vt_high = sem("vt_high")
        vt_low = sem("vt_low")
        w1_loaded = sem("w1_loaded")
        w1_high = sem("w1_high")
        w1_split = sem("w1_split")
        rope_stored = [sem(f"rope_stored_{s}") for s in range(2)]
        v_stored = [sem(f"v_stored_{s}") for s in range(2)]
        qk_loaded = [sem(f"qk_loaded_{s}") for s in range(2)]

        class At:
            pass

        def phase(k):
            p = At()
            p.k, p.blocks, p.l1 = k, FFN_BLOCKS[k], FFN_BLOCKS[k] > 1
            p.g0, p.n0 = CHUNKS * sum(FFN_BLOCKS[:k]), sum(FFN_BLOCKS[:k])
            p.pre = k in PRE
            p.s0 = p.g0 + CHUNKS * sum(j in PRE for j in range(k + 1))
            p.tab = 1 if p.l1 else 0
            p.xb0 = CHUNKS * BLOCKS if k == 3 else 0
            p.last = "final" if k == 3 else "last"
            return p

        def walk(p, engine, step):
            def at(blk, c, par, kind):
                return p.g0 + CHUNKS * blk + c, p.s0 + CHUNKS * blk + c, c, blk, par, kind

            def block_steps(blk, par, kind, before):
                prev = None
                if before:
                    prev = at(blk - 1, CHUNKS - 1, 1 - par, before)
                step(at(blk, 0, par, kind), prev)
                with engine.Fori(1, CHUNKS) as c:
                    step(at(blk, c, par, kind), at(blk, c - 1, par, kind))

            par0, last = p.n0 % 2, p.blocks - 1
            block_steps(0, par0, p.last if last == 0 else "inner", None)
            if p.blocks > 1:
                with engine.Fori(0, (p.blocks - 2) // 2) as i:
                    block_steps(1 + 2 * i, 1 - par0, "inner", "inner")
                    block_steps(2 + 2 * i, par0, "inner", "inner")
                block_steps(last, (par0 + last) % 2, p.last, "inner")

        def tail(p):
            return (p.g0 + CHUNKS * p.blocks - 1, p.s0 + CHUNKS * p.blocks - 1, CHUNKS - 1,
                    p.blocks - 1, 0, p.last)

        def positive(v):
            return not isinstance(v, int) or v > 0

        def wait(e, semaphore, v):
            if positive(v):
                e.wait_ge(semaphore, v)

        def wait_apart(e, *waits):
            for _, v in waits:
                if not isinstance(v, int):
                    e.compute_val(v)
            e.wait_ge(in_loaded, 16 * N_IN)
            for semaphore, v in waits:
                wait(e, semaphore, v)

        def pe_transpose_chunk(pe, s):
            pe.wait_ge(xn_ready, s + 1)
            wait(pe, aff_done, s)
            for k in range(KD):
                for t in range(TPC):
                    last = nc.tensor.transpose(ps[:, TPS + k, t * PART:(t + 1) * PART],
                                               xn[:, t, k * PART:(k + 1) * PART], ident[:])
            last.then_inc(tr_ready, 1)

        def pe_step(pe, p, at, prev):
            g, s, c, blk, par, kind = at
            pe.wait_ge(w_split, 4 * (p.n0 + blk + 1))
            pe.wait_ge(xT_ready, s - CHUNKS + 1)

            def mm1(j):
                wait(pe, gelu_done, HT * g + j + 1 - 4)
                first = True
                for wp, xp in PARTS:
                    for k in range(KD):
                        last = nc.tensor.matmul(
                            ps[:, HPS + j % 4, :],
                            w[par][:, wp, 0, k * HIDDEN + j * PART:k * HIDDEN + (j + 1) * PART],
                            xT[:, xp, k, bass.ds(c * CHUNK, CHUNK)], start=first,
                            stop=(wp, xp) == (0, 0) and k == KD - 1)
                        first = False
                last.then_inc(hid_ready, 1)

            def mm2(j):
                if j == 0:
                    wait(pe, y_free, g)
                pe.wait_ge(low_done, HT * g + j + 1)
                for t in range(TPC):
                    for n, (hp, wp) in enumerate(PARTS):
                        last = nc.tensor.matmul(
                            y_ps[:, t, :], hid[:, hp, j % 4, t * PART:(t + 1) * PART],
                            w[par][:, wp, 1, j * DIM:(j + 1) * DIM],
                            start=j == 0 and n == 0 and t % 2 == 0, stop=j == HT - 1 and n == 2,
                            skip_group_check=True)
                last.then_inc(mm2_done, 1)

            for j in range(HT + LAG):
                if j < HT:
                    mm1(j)
                if j >= LAG:
                    mm2(j - LAG)
                if j == 4 and prev is not None and prev[5] != "final":
                    pe_transpose_chunk(pe, prev[1])

        def act_affine(act, s, c, row):
            wait_apart(act, (tr_ready, s + 1),
                       (xT_ready, s))
            for k in range(KD):
                last = nc.scalar.activation(xTf[:, k, :], ps[:, TPS + k, :], ACT.Identity,
                                            bias=bT[:, bass.ds(row * KD + k, 1)],
                                            scale=gT[:, bass.ds(row * KD + k, 1)])
            last.then_inc(aff_done, 1)
            wait_apart(act, (aff_done, s + 1))
            nc.scalar.activation(xT[:, 0, :, bass.ds(c * CHUNK, CHUNK)], xTf[:], ACT.Copy)\
                .then_inc(xTh_done, 1)

        def act_step(act, p, at, prev):
            g, s, c, blk, par, kind = at

            def gelu(j):
                wait_apart(act, (hid_ready, HT * g + j + 1),
                           (low_done, HT * g + j + 1 - 4))
                nc.scalar.activation(gel[:, j % 4, :], ps[:, HPS + j % 4, :], ACT.Gelu,
                                     bias=b1[:, bass.ds((p.tab + blk) * HT + j, 1)]).then_inc(gelu_done, 1)

            def high(j):
                act.wait_ge(gelu_done, HT * g + j + 1)
                wait(act, mm2_done, HT * g + j + 1 - 4)
                nc.scalar.activation(hid[:, 0, j % 4, :], gel[:, j % 4, :], ACT.Copy).then_inc(round_done, 1)

            for j in range(HT + 1):
                if j < HT:
                    gelu(j)
                if j >= 1:
                    high(j - 1)
                if j == 5 and prev is not None and prev[5] != "final":
                    act_affine(act, prev[1], prev[2], prev[3] + 1 if prev[5] == "inner" else 0)

        NORM_LINKS = 14

        def dve_take(dve, p, at):
            g, s, c, blk, par, kind = at
            tiles = bass.ds(c * TPC, TPC)
            dve.wait_ge(mm2_done, HT * g + HT)
            if p.l1:
                dve.wait_ge(xb_ready, p.xb0 + CHUNKS * blk + c + 1)
                add = xb[:, tiles, :]
            else:
                add = rows[:, B2_0:B2_0 + 1, :].broadcast_to([PART, TPC, DIM])
            nc.vector.tensor_tensor(rb[:], y_ps[:, :, :], add, ALU.add).then_inc(y_free, 1)
            dve.wait_ge(y_free, g + 1)
            if kind != "inner":
                nc.vector.scalar_tensor_tensor(x[:, tiles, :], rb[:], 0.5, x[:, tiles, :], ALU.mult, ALU.add)\
                    .then_inc(x_updated, 1)
                wait_apart(dve, (x_updated, CHUNKS * p.k + c + 1 + (CHUNKS if p.k == 3 else 0)))

        def dve_norm(dve, s, c, inner, xb_made):
            n = [0]

            def link(ins):
                n[0] += 1
                ins.then_inc(dve_link, 1)
                if n[0] == 1:
                    wait_apart(dve, (dve_link, s * NORM_LINKS + 1))
                else:
                    dve.wait_ge(dve_link, s * NORM_LINKS + n[0])

            def src(t):
                return rb[:, t, :] if inner else x[:, bass.ds(c * TPC + t, 1), :]

            for t in range(TPC):
                last = nc.vector.bn_stats(stats[:, t, :], src(t))
            link(last)
            for t in range(TPC):
                last = nc.vector.bn_aggr(mv[:, t, :], stats[:, t, :])
            link(last)
            link(nc.vector.tensor_scalar(var[:], mv[:, :, 1], EPS, None, ALU.add))
            link(nc.vector.tensor_scalar(nt[:].bitcast(i32), var[:].bitcast(i32), 1, None,
                                         ALU.logical_shift_right))
            link(nc.vector.tensor_scalar(rstd[:].bitcast(i32), nt[:].bitcast(i32), -1.0,
                                         float(RSQRT_GUESS), ALU.mult, ALU.add))
            for _ in range(3):
                link(nc.vector.tensor_tensor(nt[:], rstd[:], rstd[:], ALU.mult))
                link(nc.vector.scalar_tensor_tensor(nt[:], nt[:], -0.5, var[:], ALU.mult, ALU.mult))
                link(nc.vector.scalar_tensor_tensor(rstd[:], nt[:], 1.5, rstd[:], ALU.add, ALU.mult))
            assert n[0] == NORM_LINKS
            wait(dve, tr_ready, s)
            wait(dve, xb_ready, xb_made)
            for t in range(TPC):
                last = nc.vector.tensor_scalar(xn[:, t, :], src(t), mv[:, t, 0:1], rstd[:, t:t + 1],
                                               ALU.subtract, ALU.mult)
            last.then_inc(xn_ready, 1)

        def dve_low_input(dve, s, c):
            dve.wait_ge(xTh_done, s + 1)
            chunk = bass.ds(c * CHUNK, CHUNK)
            nc.vector.tensor_tensor(xT[:, 1, :, chunk], xTf[:], xT[:, 0, :, chunk].bitcast(f32),
                                    ALU.subtract).then_inc(xT_ready, 1)

        def dve_step(dve, p, at, prev):
            g, s, c, blk, par, kind = at

            def low(j):
                dve.wait_ge(round_done, HT * g + j + 1)
                nc.vector.tensor_tensor(hid[:, 1, j % 4, :], gel[:, j % 4, :],
                                        hid[:, 0, j % 4, :].bitcast(f32), ALU.subtract).then_inc(low_done, 1)

            for j in range(HT):
                if prev is not None:
                    if j == 0:
                        dve_take(dve, p, prev)
                    if prev[5] != "final":
                        if j == 2:
                            dve_norm(dve, prev[1], prev[2], prev[5] == "inner", xb_before(p, prev))
                        if j == 6:
                            dve_low_input(dve, prev[1], prev[2])
                low(j)

        def pool_xb(pool, s, c, blk, scaled):
            wait_apart(pool, (xn_ready, s + 1))
            tiles = bass.ds(c * TPC, TPC)

            def row(r):
                return rows[:, bass.ds(r, 1), :].broadcast_to([PART, TPC, DIM])

            if blk is None:
                nc.gpsimd.tensor_tensor(xb[:, tiles, :], xn[:], row(B2_1), ALU.add).then_inc(xb_ready, 1)
            else:
                nc.gpsimd.tensor_tensor(xb[:, tiles, :], xn[:], row(GAIN + blk), ALU.mult)\
                    .then_inc(xb_scaled, 1)
                wait_apart(pool, (xb_scaled, scaled + 1))
                nc.gpsimd.tensor_tensor(xb[:, tiles, :], xb[:, tiles, :], row(B2_1 + 1 + blk), ALU.add)\
                    .then_inc(xb_ready, 1)

        def pool_split(pool, n, q, par):
            if q == 0:
                wait_apart(pool, (w_loaded, 16 * (n + 1)),
                           (mm2_done, (n - 1) * (HT * CHUNKS)))
            half, cols = q // 2, slice(q % 2 * HIDDEN, (q % 2 + 1) * HIDDEN)
            nc.gpsimd.tensor_copy(w[par][:, 0, half, cols], wraw[:, half, cols]).then_inc(w_high, 1)
            pool.wait_ge(w_high, n * 4 + q + 1)
            nc.gpsimd.tensor_tensor(w[par][:, 1, half, cols], wraw[:, half, cols],
                                    w[par][:, 0, half, cols].bitcast(f32), ALU.subtract).then_inc(w_split, 1)

        def pool_post(pool, p, at):
            g, s, c, blk, par, kind = at
            if p.k == 1:
                pool_xb(pool, s, c, None, None)
            elif p.l1 and kind == "inner":
                pool_xb(pool, s, c, blk, CHUNKS * blk + c + (CHUNKS * (BLOCKS - 1) if p.k == 3 else 0))

        def pool_step(pool, p, at, prev):
            g, s, c, blk, par, kind = at
            if prev is not None:
                pool_post(pool, p, prev)
            if kind == "inner" or p.k == 1:
                if isinstance(c, int):
                    pool_split(pool, p.n0 + blk + 1, 0, 1 - par)
                    pool_split(pool, p.n0 + blk + 1, 1, 1 - par)
                    pool_split(pool, p.n0 + blk + 1, 2, 1 - par)
                    pool_split(pool, p.n0 + blk + 1, 3, 1 - par)

        def xb_before(p, at):
            g, s, c, blk, par, kind = at
            if p.k == 0:
                return 0
            if p.k == 1:
                return c
            if p.k == 2:
                return CHUNKS + CHUNKS * blk + c if kind == "inner" else CHUNKS * BLOCKS
            return CHUNKS * BLOCKS + CHUNKS + CHUNKS * blk + c

        S_PS, AV_PS, MISC_PS = 0, 6, 7
        T_BANKS = ((4, 5, 7), (4, 5))

        ORDER = (
            dict(
                pe=("t2 s0' s1' m0 t3 s2' m1 s3' t4 t5 m2 m3 t6 t7 s4' m4 t8 m5 t9 s5' t10 "
                   "t11 m6 m7 s6' m8 s7' m9 t0' m10 m11 t1'"),
                act=("high2 n7 high3 exp0' high4 high5 c0 exp1' high6 exp2' high7 exp3' high8 "
                   "high9 exp4' high10 high11 exp5' exp6' high0' c1 exp7' high1'"),
                dve=("n6 low2 max0' max1' max2' low3 max3' low4 inv0' low5 inv1' c0 low6 max4' "
                   "n0' low7 inv2' low8 n1' n2' max5' low9 inv3' inv4' n3' low10 max6' inv5' "
                   "max7' low11 n4' inv6' low0' c1 n5' inv7' low1'"),
            ),
            dict(
                pe=("wo1- m8- s4 t11- s5 m9- m10- m11- t0 t1 s6 wo2- s7 t2 t3 wo3- m0 m1 q0' "
                   "t4 m2 m3 q1' t5 t6 s0' wo0 s1' t7 m4 m5 t8 t9 s2' m6 m7 s3' t10"),
                act=("exp0 high10- exp1 exp2 exp3 high11- exp4 c1- high0 exp5 high1 exp6 high2 "
                   "high3 exp7 q0' high4 c0 q1' high5 high6 high7 high8 high9"),
                dve=("low6- low7- low8- inv4- wo0- low9- max0 max1 max2 max3 low10- max4 "
                   "low11- inv5- inv6- inv7- wo1- max5 inv0 c1- low0 low1 max6 wo2- max7 "
                   "low2 inv1 wo3- low3 q0' inv2 inv3 low4 c0 q1' low5"),
            ),
        )

        BY_ACT = [int(word[1]) for word in ORDER[0]["act"].split() if word[0] == "n"]
        BY_DVE = [qt for qt in range(QT) if qt not in BY_ACT]

        def in_order(kind, engine):
            todo = []
            for h in range(-1, GROUP + 1):
                for word in ORDER[kind][engine].split():
                    item = word.strip("'-0123456789")
                    head = h + word.count("'") - word.count("-")
                    if 0 <= head < GROUP:
                        todo.append((item, head, int(word[len(item):].strip("'-"))))
            return todo

        SHARED = [(which, 0, half) for which in "kv" for half in range(2)] \
            + [item for item in in_order(1, "pe") if item[0] in ("q", "wo")]
        assert len(SHARED) == A1_MISC and SHARED[4:] == [item for item in in_order(1, "dve") if item[0] in ("q", "wo")]

        Q_PROJECTED = [SHARED.index(("q", h, 1)) + 1 for h in range(GROUP)]
        WO_DONE = {(h, qc): SHARED.index(("wo", h, 2 * qc + 1)) + 1 for h in range(GROUP) for qc in range(2)}

        def score_banks(qt):
            return (S_PS + qt, 1) if qt < 4 else (S_PS + 2 * (qt % 2), 2)

        def score_view(qt):
            bank, n = score_banks(qt)
            return ps[:, bank:bank + n, :].rearrange("p b n -> p (b n)")[:, 0:(qt + 1) * PART]

        BANK_USED = {0: -1, 1: -1, 2: 0, 3: 0, 4: 2, 5: 4, 6: 5, 7: 6}

        def key_tile(m):
            qc, kt = (0, m) if m < 4 else (1, m - 4)
            return qc, kt, max(0, kt - 4 * qc)

        def group_loop(e, kind, body):
            with e.Fori(0, BATCH) as b:
                with e.Fori(0, GROUPS // BATCH) as g:
                    i1 = b * (GROUPS // BATCH) + g
                    body(i1 + GROUPS * kind, i1, b, g)

        def a1_piece(part, which, h=0, k=0):
            at = {"k": 0, "v": 1, "q": 2 + h, "o": 6 + h}[which] * DIM
            if which == "o":
                return w_a1[:, part, at:at + DIM]
            return w_a1[:, part, at + k * HD1:at + (k + 1) * HD1]

        A1_PIECE = {"k": 0, "v": 1, "q": 2, "o": 6}

        def pe_att(pe, kind, i, i1, b, g):
            ql = q_sb if kind else q_st
            misc0 = A1_MISC * i1

            def scores(h, qt):
                u, width = GROUP * i + h, (qt + 1) * PART
                if not (h == 0 and qt < 4):
                    pe.wait_ge(exp_done, QT * u + BANK_USED[qt])
                if qt == 0:
                    if kind:
                        pe.wait_ge(misc_free, misc0 + Q_PROJECTED[h])
                    else:
                        pe.wait_ge(qk_loaded[h % 2], 128 * (2 * i + h // 2 + 1))
                base = score_banks(qt)[0]
                for bank in range((width + CHUNK - 1) // CHUNK):
                    n = min(CHUNK, width - bank * CHUNK)
                    dst = ps[:, base + bank, 0:n]
                    q, k = slice(qt * PART, (qt + 1) * PART), slice(bank * CHUNK, bank * CHUNK + n)
                    diagonal = bank == qt // 4
                    if kind:
                        for x3, (qp, kp) in enumerate(PARTS):
                            last = nc.tensor.matmul(dst, q_sb[:, h % 2, qp, q], k_sb[:, kp, k],
                                                    start=x3 == 0, stop=x3 == 2 and not diagonal)
                    else:
                        last = nc.tensor.matmul(dst, q_st[:, h % 2, q], k_st[:, h % 2, k],
                                                start=True, stop=not diagonal)
                    if diagonal:
                        last = nc.tensor.matmul(ps[:, base + bank, n - PART:n], ident_b[:], mask_b[:],
                                                start=False, stop=True)
                last.then_inc(s_ready, 1)

            def transpose(h, m):
                u, (qc, kt, q0) = GROUP * i + h, key_tile(m)
                if kt == 0:
                    if kind:
                        pe.wait_ge(exp_done, QT * u + 4 * qc + 4)
                    else:
                        for done, mine in ((p_by_act, BY_ACT), (p_by_dve, BY_DVE)):
                            pe.wait_ge(done, len(mine) * u + sum(qt < 4 * qc + 4 for qt in mine))
                banks = T_BANKS[kind]
                if not (h == 0 and m < len(banks)):
                    pe.wait_ge(pt_low, 12 * u + m + 1 - len(banks))
                p = p_hi if qc else p_lo
                for qi in range(q0, TPC):
                    last = nc.tensor.transpose(ps[:, banks[m % len(banks)], qi * PART:(qi + 1) * PART],
                                               p[:, qi, kt * PART:(kt + 1) * PART], ident[:])
                last.then_inc(pt_ready, 1)

            def product(h, m):
                u, (qc, kt, q0) = GROUP * i + h, key_tile(m)
                if kind == 0 and h == 0 and m == 0:
                    pe.wait_ge(v_loaded, 16 * (i + 1))
                pe.wait_ge(pt_low, 12 * u + m + 1)
                if kt == 0 and not (h == 0 and qc == 0):
                    pe.wait_ge(ctx_low, 2 * u + qc)
                cols = slice(q0 * PART, CHUNK)
                passes = ([(v_sb[:, vp, kt, :], pp) for vp, pp in PARTS] if kind
                          else [(v_st[:, kt, :], 1), (v_st[:, kt, :], 0)])
                for n, (v, pp) in enumerate(passes):
                    last = nc.tensor.matmul(ps[:, AV_PS, cols], v, pT[:, pp, m % PT_SLOTS, cols],
                                            start=kt == 0 and n == 0,
                                            stop=kt == 3 + 4 * qc and n == len(passes) - 1)
                last.then_inc(av_done, 1)

            def project(which, h, half):
                n = SHARED.index((which, h, half))
                pe.wait_ge(w1_split, 10 * i1 + A1_PIECE[which] + h + 1)
                if n:
                    pe.wait_ge(misc_free, misc0 + n)
                first = True
                for wp, xp in PARTS:
                    for k in range(KD):
                        last = nc.tensor.matmul(ps[:, MISC_PS, :], a1_piece(wp, which, h, k),
                                                xT[:, xp, k, bass.ds(b * SEQ + half * CHUNK, CHUNK)],
                                                start=first, stop=(wp, xp) == (0, 0) and k == KD - 1)
                        first = False
                last.then_inc(misc_ready, 1)

            def v_transpose(r):
                pe.wait_ge(misc_free, misc0 + 3 + r)
                for t in range(TPC):
                    last = nc.tensor.transpose(ps[:, T_BANKS[1][r], t * PART:(t + 1) * PART],
                                               xTf[:, r, t * PART:(t + 1) * PART], ident[:])
                last.then_inc(vt_ready, 1)

            def out_tiles(bank, t0, weight, done):
                for t in range(2):
                    for n, (cp, wp) in enumerate(PARTS):
                        last = nc.tensor.matmul(ps[:, bank, t * DIM:(t + 1) * DIM],
                                                ctxT[:, cp, (t0 + t) * PART:(t0 + t + 1) * PART], weight(wp),
                                                start=t == 0 and n == 0, stop=n == 2, skip_group_check=True)
                last.then_inc(done, 1)

            def output(h, r):
                pe.wait_ge(ctx_low, 2 * (GROUP * i + h) + r // 2 + 1)
                pe.wait_ge(misc_free, misc0 + SHARED.index(("wo", h, r)))
                pe.wait_ge(w1_split, 10 * i1 + 6 + h + 1)
                out_tiles(MISC_PS, 2 * r, lambda wp: a1_piece(wp, "o", h), misc_ready)

            if kind:
                for which, h, half in SHARED[:4]:
                    project(which, h, half)
                for r in range(2):
                    v_transpose(r)
            for item, h, n in in_order(kind, "pe"):
                if item == "s":
                    scores(h, n)
                elif item == "t":
                    transpose(h, n)
                elif item == "m":
                    product(h, n)
                elif item == "q":
                    project("q", h, n)
                elif item == "wo":
                    output(h, n)
            if kind == 0:
                pe.wait_ge(ctx_low, 2 * GROUP * (i + 1))
                for r in range(4):
                    if r >= 2:
                        pe.wait_ge(out_added, 4 * i + r - 1)
                    out_tiles((MISC_PS, AV_PS)[r % 2], 2 * r,
                              lambda wp: w_a0[:, wp, bass.ds(g * DIM + 5 * KD * DIM, DIM)], out_ready)
                pe.wait_ge(out_added, 4 * (i + 1))
            if kind:
                pe.wait_ge(misc_free, misc0 + A1_MISC)

        def act_att(act, kind, i, i1, b, g):
            misc0 = A1_MISC * i1

            def exp(h, qt):
                u = GROUP * i + h
                act.wait_ge(max_ready, QT * u + qt + 1)
                if h:
                    act.wait_ge(pt_ready, 12 * (u - 1) + (12 if qt >= 4 else 4))
                p = p_hi if qt >= 4 else p_lo
                nc.scalar.activation(p[:, qt % 4, 0:(qt + 1) * PART], score_view(qt), ACT.Exp,
                                     bias=negmax[:, qt:qt + 1],
                                     accum_out=rowsum[:, h % 2, qt:qt + 1]).then_inc(exp_done, 1)

            def high(h, m):
                u, q0 = GROUP * i + h, key_tile(m)[2]
                act.wait_ge(pt_ready, 12 * u + m + 1)
                if not (h == 0 and m < PT_SLOTS):
                    act.wait_ge(av_done, 12 * u + m + 1 - PT_SLOTS)
                nc.scalar.activation(pT[:, 0, m % PT_SLOTS, q0 * PART:],
                                     ps[:, T_BANKS[kind][m % len(T_BANKS[kind])], q0 * PART:],
                                     ACT.Copy).then_inc(pt_high, 1)

            def ctx_part(h, qc):
                u, cols = GROUP * i + h, slice(qc * CHUNK, (qc + 1) * CHUNK)
                act.wait_ge(av_done, 12 * u + 4 + 8 * qc)
                if kind and h:
                    act.wait_ge(misc_ready, misc0 + WO_DONE[h - 1, qc])
                mine = slice(0, PART) if kind else slice(32 * h, 32 * h + 32)
                nc.scalar.activation(ctxT[mine, 0, cols], ps[mine, AV_PS, :], ACT.Copy).then_inc(ctx_high, 1)

            def normalise(h, qt):
                act.wait_ge(inv_ready, QT * (GROUP * i + h) + qt + 1)
                p = (p_hi if qt >= 4 else p_lo)[:, qt % 4, 0:(qt + 1) * PART]
                nc.scalar.activation(p, p, ACT.Copy, scale=rowinv[:, h % 2, qt:qt + 1]).then_inc(p_by_act, 1)

            def projected(which, h, half):
                act.wait_ge(misc_ready, misc0 + SHARED.index((which, h, half)) + 1)
                dst = (k_sb[:, 0, :] if which == "k" else q_sb[:, h % 2, 0, :])
                nc.scalar.activation(dst[:, half * CHUNK:(half + 1) * CHUNK], ps[:, MISC_PS, :],
                                     ACT.Copy).then_inc(misc_high, 1)

            if kind:
                for half in range(2):
                    projected("k", 0, half)
                for r in range(2):
                    act.wait_ge(vt_ready, 2 * i1 + r + 1)
                    nc.scalar.activation(v_sb[:, 0, 4 * r:4 * r + 4, :].rearrange("p t n -> p (t n)"),
                                         ps[:, T_BANKS[1][r], :], ACT.Copy).then_inc(vt_high, 1)
            for item, h, n in in_order(kind, "act"):
                if item == "exp":
                    exp(h, n)
                elif item == "high":
                    high(h, n)
                elif item == "c":
                    ctx_part(h, n)
                elif item == "n":
                    normalise(h, n)
                elif item == "q":
                    projected("q", h, n)

        def dve_att(dve, kind, i, i1, b, g):
            misc0 = A1_MISC * i1

            def maximum(h, qt):
                dve.wait_ge(s_ready, QT * (GROUP * i + h) + qt + 1)
                nc.vector.tensor_reduce(negmax[:, qt:qt + 1], score_view(qt), AX.X, ALU.max,
                                        negate=True).then_inc(max_ready, 1)

            def inverse(h, qt):
                dve.wait_ge(exp_done, QT * (GROUP * i + h) + qt + 1)
                nc.vector.reciprocal(rowinv[:, h % 2, qt:qt + 1], rowsum[:, h % 2, qt:qt + 1])\
                    .then_inc(inv_ready, 1)

            def low(h, m):
                q0 = key_tile(m)[2]
                dve.wait_ge(pt_high, 12 * (GROUP * i + h) + m + 1)
                nc.vector.tensor_tensor(pT[:, 1, m % PT_SLOTS, q0 * PART:],
                                        ps[:, T_BANKS[kind][m % len(T_BANKS[kind])], q0 * PART:],
                                        pT[:, 0, m % PT_SLOTS, q0 * PART:].bitcast(f32),
                                        ALU.subtract).then_inc(pt_low, 1)

            def ctx_part(h, qc):
                u, cols = GROUP * i + h, slice(qc * CHUNK, (qc + 1) * CHUNK)
                mine = slice(0, PART) if kind else slice(32 * h, 32 * h + 32)
                dve.wait_ge(ctx_high, 2 * u + qc + 1)
                nc.vector.tensor_tensor(ctxT[mine, 1, cols], ps[mine, AV_PS, :],
                                        ctxT[mine, 0, cols].bitcast(f32), ALU.subtract).then_inc(ctx_low, 1)

            def normalise(h, qt):
                dve.wait_ge(inv_ready, QT * (GROUP * i + h) + qt + 1)
                p = (p_hi if qt >= 4 else p_lo)[:, qt % 4, 0:(qt + 1) * PART]
                nc.vector.tensor_scalar(p, p, rowinv[:, h % 2, qt:qt + 1], None, ALU.mult).then_inc(p_by_dve, 1)

            def projected(which, h, half):
                n, cols = SHARED.index((which, h, half)), slice(half * CHUNK, (half + 1) * CHUNK)
                if which == "v":
                    dve.wait_ge(misc_ready, misc0 + n + 1)
                    nc.vector.tensor_copy(xTf[:, half, :], ps[:, MISC_PS, :]).then_inc(misc_free, 1)
                else:
                    dve.wait_ge(misc_high, 10 * i1 + (2 + 2 * h if which == "q" else 0) + half + 1)
                    whole, rest = ((k_sb[:, part, cols] if which == "k" else q_sb[:, h % 2, part, cols])
                                   for part in (0, 1))
                    nc.vector.tensor_tensor(rest, ps[:, MISC_PS, :], whole.bitcast(f32), ALU.subtract)\
                        .then_inc(misc_free, 1)

            def add_head(h, r):
                dve.wait_ge(misc_ready, misc0 + SHARED.index(("wo", h, r)) + 1)
                dve.wait_ge(inv_ready, QT * (GROUP * i + h) + 2 * r + 2)
                for t in range(2):
                    dst = x[:, bass.ds(b * QT + 2 * r + t, 1), :].rearrange("p o e -> p (o e)")
                    last = nc.vector.scalar_tensor_tensor(dst, ps[:, MISC_PS, t * DIM:(t + 1) * DIM],
                                                          rowinv[:, h % 2, 2 * r + t:2 * r + t + 1], dst,
                                                          ALU.mult, ALU.add)
                last.then_inc(misc_free, 1)

            def add_out(bank, t0):
                dst = x[:, bass.ds(b * QT + t0, 2), :]
                nc.vector.tensor_tensor(dst, ps[:, bank, :].rearrange("p (t e) -> p t e", t=2), dst,
                                        ALU.add).then_inc(out_added, 1)

            if kind:
                for which, h, half in SHARED[:4]:
                    projected(which, h, half)
                for r in range(2):
                    dve.wait_ge(vt_high, 2 * i1 + r + 1)
                    whole, rest = (v_sb[:, part, 4 * r:4 * r + 4, :].rearrange("p t n -> p (t n)") for part in (0, 1))
                    nc.vector.tensor_tensor(rest, ps[:, T_BANKS[1][r], :], whole.bitcast(f32), ALU.subtract)\
                        .then_inc(vt_low, 1)
            for item, h, n in in_order(kind, "dve"):
                if item == "max":
                    maximum(h, n)
                elif item == "inv":
                    inverse(h, n)
                elif item == "low":
                    low(h, n)
                elif item == "c":
                    ctx_part(h, n)
                elif item == "n":
                    normalise(h, n)
                elif item == "q":
                    projected("q", h, n)
                elif item == "wo":
                    add_head(h, n)
            if kind == 0:
                for r in range(4):
                    dve.wait_ge(out_ready, 4 * i + r + 1)
                    add_out((MISC_PS, AV_PS)[r % 2], 2 * r)

        def last_use(piece):
            return max(n + 1 for n, (which, h, _) in enumerate(SHARED)
                       if piece == A1_PIECE.get(which, A1_PIECE["o"]) + h)

        def pool_split_a1(pool, i, first):
            wait_apart(pool, (w1_loaded, 16 * (i + 1)))
            for piece in range(10):
                cols = slice(piece * DIM, (piece + 1) * DIM)
                if not first:
                    wait_apart(pool, (misc_ready, A1_MISC * (i - 1) + last_use(piece)))
                nc.gpsimd.tensor_copy(w_a1[:, 0, cols], xb[:, piece, :]).then_inc(w1_high, 1)
                pool.wait_ge(w1_high, 10 * i + piece + 1)
                nc.gpsimd.tensor_tensor(w_a1[:, 1, cols], xb[:, piece, :], w_a1[:, 0, cols].bitcast(f32),
                                        ALU.subtract).then_inc(w1_split, 1)

        PIECES = [(qk, half) for qk in range(2) for half in range(KD)]
        V_W = 4 * KD * DIM

        def a0_raw(piece):
            bounds = [0, 2 * KD * DIM, 4 * KD * DIM, A0_W]
            return slice(bounds[piece], bounds[piece + 1])

        xb_flat = xb[:, :, :].rearrange("p t e -> p (t e)")

        def rope_pieces(e, body):
            with e.Fori(0, BATCH) as b:
                for m in range(2 * len(PIECES)):
                    sc, (qk, half) = m // len(PIECES), PIECES[m % len(PIECES)]
                    body(b * (2 * len(PIECES)) + m, b * SEQ + sc * CHUNK, sc * CHUNK, qk, half, m % 2, m, b * len(PIECES) + m // 2)

        def pe_project_a0(pe):
            pe.wait_ge(xT_ready, S_ATT[0])

            def piece(n, token, seq, qk, half, slot, m, half_n):
                if m >= 2:
                    pe.wait_ge(rope_taken, n - 1)
                for swap in range(2):
                    pe.wait_ge(a_low, qk + 1)
                    first = True
                    for wp, xp in PARTS:
                        for k in range(KD):
                            at = ((2 * qk + swap) * KD + k) * DIM + half * PART
                            last = nc.tensor.matmul(ps[:, 2 * slot + swap, :], w_a0[:, wp, at:at + PART],
                                                    xT[:, xp, k, bass.ds(token, CHUNK)], start=first,
                                                    stop=(wp, xp) == (0, 0) and k == KD - 1)
                            first = False
                last.then_inc(proj_ready, 1)
                if m == 2 * len(PIECES) - 1:
                    pe.wait_ge(rope_taken, n + 1)

            rope_pieces(pe, piece)
            pe.wait_ge(a_low, 3)
            for t in range(TILES):
                wait(pe, v_low, t - 1)
                first = True
                for wp, xp in PARTS:
                    for k in range(KD):
                        last = nc.tensor.matmul(ps[:, 4 + t % 2, 0:DIM],
                                                xT[:, xp, k, t * PART:(t + 1) * PART],
                                                w_a0[:, wp, V_W + k * DIM:V_W + (k + 1) * DIM], start=first,
                                                stop=(wp, xp) == (0, 0) and k == KD - 1)
                        first = False
                last.then_inc(v_ready, 1)
            pe.wait_ge(v_low, TILES)

        def act_project_a0(act):
            act.wait_ge(a_loaded, 16)
            act.wait_ge(xT_ready, S_ATT[0])
            for piece in range(3):
                nc.scalar.activation(w_a0[:, 0, a0_raw(piece)], xb_flat[:, a0_raw(piece)], ACT.Copy)\
                    .then_inc(a_high, 1)

            def piece(n, token, seq, qk, half, slot, m, half_n):
                act.wait_ge(rope_sum, n + 1)
                if m >= 2:
                    act.wait_ge(rope_stored[slot], 16 * half_n)
                nc.scalar.activation(rope_hl[:, 0, slot, :], rope[:, 2, slot, :], ACT.Copy)\
                    .then_inc(rope_high, 1)
                if m == 2 * len(PIECES) - 1:
                    for stored in rope_stored:
                        act.wait_ge(stored, 16 * (half_n + 1))

            rope_pieces(act, piece)
            for t in range(TILES):
                act.wait_ge(v_ready, t + 1)
                wait(act, v_stored[t % 2], 16 * (t // 2))
                nc.scalar.activation(v_hl[:, t % 2, :, 0, :],
                                     ps[:, 4 + t % 2, 0:DIM].rearrange("p (h d) -> p h d", h=HEADS),
                                     ACT.Copy).then_inc(v_high, 1)

        def dve_project_a0(dve):
            for piece in range(3):
                dve.wait_ge(a_high, piece + 1)
                nc.vector.tensor_tensor(w_a0[:, 1, a0_raw(piece)], xb_flat[:, a0_raw(piece)],
                                        w_a0[:, 0, a0_raw(piece)].bitcast(f32), ALU.subtract)\
                    .then_inc(a_low, 1)
            dve.wait_ge(a_low, 3)
            dve.wait_ge(att_tab, 16)

            def piece(n, token, seq, qk, half, slot, m, half_n):
                dve.wait_ge(proj_ready, n + 1)
                for term in range(2):
                    nc.vector.tensor_tensor(rope[:, term, slot, :], ps[:, 2 * slot + term, :],
                                            rot[:, 2 * qk + term, seq:seq + CHUNK], ALU.mult)\
                        .then_inc((rope_term, rope_taken)[term], 1)
                dve.wait_ge(rope_taken, n + 1)
                nc.vector.tensor_tensor(rope[:, 2, slot, :], rope[:, 0, slot, :], rope[:, 1, slot, :],
                                        ALU.add).then_inc(rope_sum, 1)
                dve.wait_ge(rope_high, n + 1)
                nc.vector.tensor_tensor(rope_hl[:, 1, slot, :], rope[:, 2, slot, :],
                                        rope_hl[:, 0, slot, :].bitcast(f32), ALU.subtract)\
                    .then_inc(rope_low, 1)

            rope_pieces(dve, piece)
            for t in range(TILES):
                dve.wait_ge(v_high, t + 1)
                nc.vector.tensor_tensor(v_hl[:, t % 2, :, 1, :],
                                        ps[:, 4 + t % 2, 0:DIM].rearrange("p (h d) -> p h d", h=HEADS),
                                        v_hl[:, t % 2, :, 0, :].bitcast(f32), ALU.subtract)\
                    .then_inc(v_low, 1)

        def sp_project_a0(sp):
            sp.wait_ge(xT_ready, S_ATT[0])
            sp.dma_start(xb_flat[:, 0:A0_W], a["w_a0"]).then_inc(a_loaded, 16)
            sp.dma_start(rot[:], a["rot"]).then_inc(att_tab, 16)

            def piece(n, token, seq, qk, half, slot, m, half_n):
                wait_apart(sp, (rope_low, n + 1))
                sp.dma_start(qk_dram[qk, half * PART:(half + 1) * PART, :, bass.ds(token, CHUNK)],
                             rope_hl[:, :, slot, :].bitcast(f32)).then_inc(rope_stored[slot], 16)

            rope_pieces(sp, piece)
            for t in range(TILES):
                sp.wait_ge(v_low, t + 1)
                sp.dma_start(v_dram[t, :, :],
                             v_hl[:, t % 2, :, :, :].rearrange("p h a d -> p (h a d)").bitcast(f32))\
                    .then_inc(v_stored[t % 2], 16)
            for stored in rope_stored:
                sp.wait_ge(stored, 16 * 2 * len(PIECES))
            for stored in v_stored:
                sp.wait_ge(stored, 16 * TILES // 2)

            def group(i, i1, b, g):
                for h in range(GROUP):
                    u = GROUP * i + h
                    if h >= 2:
                        wait_apart(sp, (s_ready, QT * (u - 1)))
                    for row, (qp, kp) in enumerate(((0, 0), (1, 0), (0, 1), (1, 1))):
                        for dst, qk, part in ((q_st, 0, qp), (k_st, 1, kp)):
                            sp.dma_start(dst[row * HD0:(row + 1) * HD0, h % 2, :].bitcast(f32),
                                         qk_dram[qk, bass.ds((GROUP * g + h) * HD0, HD0), part,
                                                 bass.ds(b * SEQ, SEQ)]).then_inc(qk_loaded[h % 2], 16)
                    if h == 0:
                        sp.dma_start(v_st[:].bitcast(f32), v_dram[bass.ds(b * QT, QT), :, bass.ds(g * PART, PART)]
                                     .rearrange("t p n -> p t n")).then_inc(v_loaded, 16)
                wait_apart(sp, (av_done, 12 * GROUP * (i + 1)))

            group_loop(sp, 0, group)

        def attention(e, kind, body):
            group_loop(e, kind, lambda i, i1, b, g: body(e, kind, i, i1, b, g))

        ATT_END = {0: (out_added, 4 * GROUPS), 1: (misc_free, A1_MISC * GROUPS)}
        S_ATT = {0: CHUNKS * 2, 1: CHUNKS * (2 + 1 + 1 + BLOCKS)}
        ATT_BEFORE = {1: 0, 3: 1}

        def x_ready(e, k):
            if k == 0:
                e.wait_ge(in_loaded, 16 * N_IN)
                e.wait_ge(tab_ready, 1)
            elif ATT_BEFORE[k] in ATTS:
                e.wait_ge(*ATT_END[ATT_BEFORE[k]])

        def pre_posts(e, k, body):
            p = phase(k)
            if p.pre:
                body(p, p.s0 - CHUNKS, 0)
                with e.Fori(1, CHUNKS) as c:
                    body(p, p.s0 - CHUNKS + c, c)

        N_IN = 9

        block = ctx.enter_context(nc.Block())

        @block.sync
        def _(sp):
            for t in range(CHUNKS):
                tiles = slice(t * TPC, (t + 1) * TPC)
                sp.dma_start(x[:, tiles, :], a["x"].rearrange("(t p) e -> p t e", p=PART)[:, tiles, :])\
                    .then_inc(in_loaded, 16)
            sp.dma_start(ident[:], a["ident"]).then_inc(in_loaded, 16)
            sp.dma_start(b1[:], a["b1"]).then_inc(in_loaded, 16)
            sp.dma_start(gT[:, KD:], a["gT"]).then_inc(in_loaded, 16)
            sp.dma_start(bT[:, KD:], a["bT"]).then_inc(in_loaded, 16)
            sp.dma_start(rows[:], a["rows"].partition_broadcast(PART)).then_inc(in_loaded, 16)
            sp.dma_start(lnb[:], a["lnb"].partition_broadcast(PART)).then_inc(lnb_loaded, 16)
            sp.dma_start(rb[:, 0, 0:PART], a["mask"]).then_inc(lnb_loaded, 16)

            def load(n, source):
                wait_apart(sp, (w_split, 4 * n))
                sp.dma_start(wraw[:], a["wffn"][bass.ds(source, 1), :, :].rearrange(
                    "o p (h n) -> p (o h) n", h=2)).then_inc(w_loaded, 16)

            for k in range(LASTK + 1):
                p = phase(k)
                if k == 1 and 0 in ATTS:
                    sp_project_a0(sp)
                if k == 3 and 1 in ATTS:
                    sp.wait_ge(xT_ready, S_ATT[1])
                    sp.dma_start(xb[:, 0:10, :], a["w_a1"][0, :, :].rearrange("p (t e) -> p t e", e=DIM))\
                        .then_inc(w1_loaded, 16)
                    with sp.Fori(1, GROUPS) as i:
                        wait_apart(sp, (w1_split, 10 * i))
                        sp.dma_start(xb[:, 0:10, :], a["w_a1"][bass.ds(i, 1), :, :].rearrange(
                            "o p (t e) -> p (o t) e", e=DIM)).then_inc(w1_loaded, 16)
                if p.pre:
                    x_ready(sp, k)
                if k != 2:
                    load(p.n0, p.tab)
                if k == 1:
                    load(p.n0 + 1, 1)
                if p.l1:
                    with sp.Fori(1, p.blocks) as blk:
                        load(p.n0 + blk, p.tab + blk)
            if FINAL:
                for c in range(CHUNKS):
                    sp.wait_ge(x_updated, 4 * CHUNKS + c + 1)
                    sp.dma_start(a["out"].rearrange("(t p) e -> p t e", p=PART)[:, c * TPC:(c + 1) * TPC, :],
                                 x[:, c * TPC:(c + 1) * TPC, :]).then_inc(out_stored, 16)
            else:
                sp.wait_ge(x_updated, CHUNKS * (LASTK + 1))
                for c in range(CHUNKS):
                    sp.dma_start(a["out"].rearrange("(t p) e -> p t e", p=PART)[:, c * TPC:(c + 1) * TPC, :],
                                 x[:, c * TPC:(c + 1) * TPC, :]).then_inc(out_stored, 16)
            sp.wait_ge(out_stored, 16 * CHUNKS)

        @block.gpsimd
        def _(pool):
            nc.gpsimd.memset(gT[:, 0:KD], 1.0)
            nc.gpsimd.memset(bT[:, 0:KD], 0.0).then_inc(tab_ready, 1)
            pool.wait_ge(in_loaded, 16 * N_IN)
            pool.wait_ge(lnb_loaded, 32)
            nc.gpsimd.tensor_copy(ident_b[:], ident[:]).then_inc(ident_ready, 1)
            nc.gpsimd.tensor_copy(mask_b[:], rb[:, 0, 0:PART]).then_inc(ident_ready, 1)
            nc.gpsimd.tensor_tensor(rows[:, B2_1 + 1:B2_1 + BLOCKS, :], rows[:, B2_1 + 1:B2_1 + BLOCKS, :],
                                    lnb[:], ALU.add).then_inc(rows_ready, 1)
            pool.wait_ge(rows_ready, 1)
            for k in range(LASTK + 1):
                p = phase(k)
                if k == 3 and 1 in ATTS:
                    pool_split_a1(pool, 0, True)
                    with pool.Fori(1, GROUPS) as i:
                        pool_split_a1(pool, i, False)
                if p.pre:
                    x_ready(pool, k)
                if k != 2:
                    for q in range(4):
                        pool_split(pool, p.n0, q, p.n0 % 2)
                if k == 3:
                    pre_posts(pool, k, lambda p, s, c: pool_xb(pool, s, c, None, None))
                walk(p, pool, lambda at, prev: pool_step(pool, p, at, prev))
                pool_post(pool, p, tail(p))

        @block.scalar
        def _(act):
            act.wait_ge(in_loaded, 16 * N_IN)
            act.wait_ge(tab_ready, 1)
            for k in range(LASTK + 1):
                p = phase(k)
                if k == 1 and 0 in ATTS:
                    act_project_a0(act)
                    attention(act, 0, act_att)
                if k == 3 and 1 in ATTS:
                    act.wait_ge(xT_ready, S_ATT[1])
                    attention(act, 1, act_att)
                pre_posts(act, k, lambda p, s, c: act_affine(act, s, c, 0))
                walk(p, act, lambda at, prev: act_step(act, p, at, prev))
                if p.last != "final":
                    act_affine(act, tail(p)[1], CHUNKS - 1, 0)

        @block.vector
        def _(dve):
            dve.wait_ge(ident_ready, 2)
            for k in range(LASTK + 1):
                p = phase(k)

                def pre(p, s, c):
                    if p.k == 3:
                        tiles = bass.ds(c * TPC, TPC)
                        nc.vector.tensor_tensor(x[:, tiles, :], x[:, tiles, :], rows[:, BO:BO + 1, :]
                                                .broadcast_to([PART, TPC, DIM]), ALU.add).then_inc(x_updated, 1)
                        wait_apart(dve, (x_updated, 3 * CHUNKS + c + 1))
                    dve_norm(dve, s, c, False, CHUNKS * BLOCKS + c if p.k == 3 else 0)
                    dve_low_input(dve, s, c)

                if k == 1 and 0 in ATTS:
                    dve_project_a0(dve)
                    attention(dve, 0, dve_att)
                if k == 3 and 1 in ATTS:
                    attention(dve, 1, dve_att)
                if p.pre:
                    x_ready(dve, k)
                pre_posts(dve, k, pre)
                walk(p, dve, lambda at, prev: dve_step(dve, p, at, prev))
                dve_take(dve, p, tail(p))
                if p.last != "final":
                    dve_norm(dve, tail(p)[1], CHUNKS - 1, False, xb_before(p, tail(p)))
                    dve_low_input(dve, tail(p)[1], CHUNKS - 1)

        @block.tensor
        def _(pe):
            pe.wait_ge(in_loaded, 16 * N_IN)
            for k in range(LASTK + 1):
                p = phase(k)
                if k == 1 and 0 in ATTS:
                    pe.wait_ge(ident_ready, 2)
                    pe_project_a0(pe)
                    attention(pe, 0, pe_att)
                if k == 3 and 1 in ATTS:
                    pe.wait_ge(xT_ready, S_ATT[1])
                    attention(pe, 1, pe_att)
                pre_posts(pe, k, lambda p, s, c: pe_transpose_chunk(pe, s))
                walk(p, pe, lambda at, prev: pe_step(pe, p, at, prev))
                if p.last != "final":
                    pe_transpose_chunk(pe, tail(p)[1])


def rotation():
    f = np.float32
    inverse = (f(1) / np.power(f(ROPE_BASE), np.arange(0, HD0, 2, dtype=f) / f(HD0))).astype(f)
    angles = np.outer(inverse, np.arange(SEQ, dtype=f)).astype(f)
    cos = np.tile(np.cos(angles), (2, 1))
    sin = np.concatenate([-np.sin(angles), np.sin(angles)])
    one = np.stack([np.tile(v, (PART // HD0, 1)) for v in (cos, sin)], axis=1)
    return np.concatenate([one * f(HD0 ** -0.5), one], axis=1).astype(f)


def layout(d):
    f = np.float32

    def columns(v):
        return np.ascontiguousarray(v.reshape(-1, PART).T)

    def ffn(w1, w2):
        one = w1.T.reshape(KD, PART, HIDDEN).transpose(1, 0, 2).reshape(PART, -1)
        two = w2.T.reshape(HT, PART, DIM).transpose(1, 0, 2).reshape(PART, -1)
        return np.concatenate([one, two], axis=1)

    def heads(w, swap=False):
        if swap:
            w = w.reshape(HEADS, 2, HD0 // 2, DIM)[:, ::-1].reshape(DIM, DIM)
        return w.T.reshape(KD, PART, DIM).transpose(1, 0, 2).reshape(PART, -1)

    wq, wk, wv, wo = (d[f"L0_attn_{n}"] for n in ("Wq", "Wk", "Wv", "Wo"))
    stack = wo.T.reshape(GROUP, GROUP, 1, HD0, DIM).repeat(2, axis=2).reshape(GROUP, PART, DIM)
    w_a0 = np.concatenate([heads(wq), heads(wq, True), heads(wk), heads(wk, True), heads(wv),
                           stack.transpose(1, 0, 2).reshape(PART, -1)], axis=1)

    def columns_of(w):
        return w.T.reshape(KD, PART, HD1).transpose(1, 0, 2).reshape(PART, -1)

    wq1, wk1, wv1, wo1 = (d[f"L1_attn_{n}"] for n in ("Wq", "Wk", "Wv", "Wo"))
    groups = []
    for n in range(KV1):
        rows = slice(n * HD1, (n + 1) * HD1)
        mine = [slice((GROUP * n + h) * HD1, (GROUP * n + h + 1) * HD1) for h in range(GROUP)]
        groups.append(np.concatenate([columns_of(wk1[rows]), columns_of(wv1[rows])]
                                     + [columns_of(wq1[r]) for r in mine] + [wo1[:, r].T for r in mine], axis=1))
    w_a1 = np.stack(groups * BATCH)

    return {
        "w_a0": w_a0, "w_a1": w_a1, "rot": rotation(), "mask": np.triu(np.full((PART, PART), MASKED, f), 1),
        "x": np.ascontiguousarray(d["L0_attn_hidden_states"].reshape(TOKENS, DIM)),
        "ident": np.eye(PART, dtype=f),
        "b1": columns(np.concatenate([d["L0_ffn_proj1_bias"][None], d["L1_ffn_B1"]])),
        "gT": columns(d["L1_ffn_LN_G"]), "bT": columns(d["L1_ffn_LN_B"]),
        "rows": np.concatenate([d["L0_ffn_proj2_bias"][None], d["L1_attn_bo"][None], d["L1_ffn_B2"],
                                d["L1_ffn_LN_G"]]),
        "lnb": np.ascontiguousarray(d["L1_ffn_LN_B"]),
        "wffn": np.stack([ffn(d["L0_ffn_proj1"], d["L0_ffn_proj2"])]
                         + [ffn(d["L1_ffn_W1"][i], d["L1_ffn_W2"][i]) for i in range(BLOCKS)]),
    }


def kernel(**inputs):
    import concourse.bacc as bacc
    from concourse.bass_utils import run_bass_kernel_spmd

    arrays = {n: v for n, v in layout({k: np.asarray(v) for k, v in inputs.items()}).items()}
    nc = bacc.Bacc("TRN2", target_bir_lowering=False, num_devices=1)
    aps = {n: nc.dram_tensor(f"in_{n}", v.shape, mybir.dt.from_np(v.dtype), kind="ExternalInput").ap()
           for n, v in arrays.items()}
    aps["out"] = nc.dram_tensor("out", (TOKENS, DIM), mybir.dt.float32, kind="ExternalOutput").ap()
    build(nc, aps)
    r = run_bass_kernel_spmd(nc, [{f"in_{n}": v for n, v in arrays.items()}], core_ids=[0])
    return r.results[0]["out"].reshape(BATCH, SEQ, DIM)
```

```python
from contextlib import ExitStack

import concourse.bass as bass
import numpy as np
from concourse import mybir
from concourse.alu_op_type import AluOpType as ALU

PART = 128
BATCH, SEQ, DIM = 2, 1024, 256
TOKENS = BATCH * SEQ
HIDDEN = 1024
BLOCKS = 6
CHUNK = 512
CHUNKS = TOKENS // CHUNK
TILES = TOKENS // PART
TPC = CHUNK // PART
KD = DIM // PART
HT = HIDDEN // PART
EPS = 1e-5
HEADS = 16
HD0 = DIM // HEADS
HD1 = 128
KV1 = 4
GROUP = 4
GROUPS = BATCH * HEADS // GROUP
QT = SEQ // PART
ROPE_BASE = 10000.0
MASKED = -1e30
RSQRT_GUESS = 0x5F3759DF
A0_W = 5 * KD * DIM + GROUP * DIM
A1_W = 10 * DIM
A1_MISC = 6 + GROUP * 6
A1_HIGHS = 4 + GROUP * 2
FFN_BLOCKS = (1, 1, BLOCKS, BLOCKS)
PHASES = len(FFN_BLOCKS)
PT_SLOTS = 4
LAG = 3
PARTS = ((1, 0), (0, 1), (0, 0))


PRE = (0, 1, 3)


def build(nc, a):
    f32, f32r, i32, bf16 = mybir.dt.float32, mybir.dt.float32r, mybir.dt.int32, mybir.dt.bfloat16
    ACT = mybir.ActivationFunctionType
    AX = mybir.AxisListType
    ctx = ExitStack()
    with ctx:
        def sb(name, shape, dt=f32, stack=ctx):
            return stack.enter_context(nc.sbuf_tensor(name, shape, dt))

        def sem(name):
            return ctx.enter_context(nc.semaphore(name))

        x = sb("x", [PART, TILES, DIM])
        xT = sb("xT", [PART, 2, KD, TOKENS], f32r)
        xb = sb("xb", [PART, TILES, DIM])
        rb = sb("rb", [PART, TPC, DIM])
        xn = sb("xn", [PART, TPC, DIM])
        xTf = sb("xTf", [PART, KD, CHUNK])
        rows = sb("rows", [PART, 1 + 2 * BLOCKS, DIM])
        B2_0, BO, B2_1, GAIN = 0, 1, 2, 2 + BLOCKS
        lnb = sb("lnb", [PART, BLOCKS - 1, DIM])
        b1 = sb("b1", [PART, (1 + BLOCKS) * HT])
        gT = sb("gT", [PART, BLOCKS * KD])
        bT = sb("bT", [PART, BLOCKS * KD])
        ident = sb("ident", [PART, PART])
        stats = sb("stats", [PART, TILES, 6])
        mv = sb("mv", [PART, TILES, 2])
        var = sb("var", [PART, TILES])
        rstd = sb("rstd", [PART, TILES])
        nt = sb("nt", [PART, TILES])
        negmax = sb("negmax", [PART, 2, QT])
        rowsum = sb("rowsum", [PART, 2, QT])
        rowinv = sb("rowinv", [PART, 2, QT])
        ident_b = sb("ident_b", [PART, PART], bf16)
        mask_b = sb("mask_b", [PART, PART], bf16)

        ffn = ExitStack()
        wraw = sb("wraw", [PART, 2, KD * HIDDEN], f32, ffn)
        w = [sb(f"w{p}", [PART, 2, 2, KD * HIDDEN], f32r, ffn) for p in range(2)]
        gel = sb("gel", [PART, 4, CHUNK], f32, ffn)
        hid = sb("hid", [PART, 2, 4, CHUNK], f32r, ffn)
        ffn.close()

        att = ExitStack()
        p_lo = sb("p_lo", [PART, TPC, SEQ // 2], f32, att)
        p_hi = sb("p_hi", [PART, TPC, SEQ], f32, att)
        pT = sb("pT", [PART, 2, PT_SLOTS, CHUNK], f32r, att)
        ctxT = sb("ctxT", [PART, 2, SEQ], f32r, att)
        q_sb = sb("q_sb", [PART, 2, 2, SEQ], f32r, att)
        k_sb = sb("k_sb", [PART, 2, SEQ], f32r, att)
        v_sb = sb("v_sb", [PART, 2, QT, HD1], f32r, att)
        w_a1 = sb("w_a1", [PART, 2, A1_W], f32r, att)
        att.close()
        att = ExitStack()
        for name, shape in (("p_lo0", [PART, TPC, SEQ // 2]), ("p_hi0", [PART, TPC, SEQ])):
            sb(name, shape, f32, att)
        sb("pT0", [PART, 2, PT_SLOTS, CHUNK], f32r, att)
        sb("ctxT0", [PART, 2, SEQ], f32r, att)
        q_st = sb("q_st", [64, 2, SEQ], f32r, att)
        k_st = sb("k_st", [64, 2, SEQ], f32r, att)
        v_st = sb("v_st", [PART, QT, PART], f32r, att)
        w_a0 = sb("w_a0", [PART, 2, A0_W], f32r, att)
        att.close()
        att = ExitStack()
        rot = sb("rot", [PART, 4, SEQ], f32, att)
        rope = sb("rope", [PART, 3, 2, CHUNK], f32, att)
        rope_hl = sb("rope_hl", [PART, 2, 2, CHUNK], f32r, att)
        v_hl = sb("v_hl", [PART, 4, HEADS, 2, HD0], f32r, att)
        att.close()

        qk_dram = nc.dram_tensor("qk_dram", (2, DIM, 2, TOKENS), f32, kind="Internal").ap()
        v_dram = nc.dram_tensor("v_dram", (TILES, PART, 2 * DIM), f32, kind="Internal").ap()
        ps = ctx.enter_context(nc.psum_tensor("ps", [PART, 8, CHUNK], f32))
        HPS, YPS, TPS = 0, 4, 6
        y_ps = ps[:, YPS:YPS + 2, :].rearrange("p b (t e) -> p (b t) e", e=DIM)

        in_loaded = sem("in_loaded")
        lnb_loaded = sem("lnb_loaded")
        tab_ready = sem("tab_ready")
        rows_ready = sem("rows_ready")
        w_loaded = sem("w_loaded")
        w_high = sem("w_high")
        w_split = sem("w_split")
        hid_ready = sem("hid_ready")
        gelu_done = sem("gelu_done")
        round_done = sem("round_done")
        low_done = sem("low_done")
        mm2_done = sem("mm2_done")
        y_free = sem("y_free")
        x_updated = sem("x_updated")
        xn_ready = sem("xn_ready")
        tr_ready = sem("tr_ready")
        aff_done = sem("aff_done")
        xTh_done = sem("xTh_done")
        xT_ready = sem("xT_ready")
        xb_scaled = sem("xb_scaled")
        xb_ready = sem("xb_ready")
        dve_link = sem("dve_link")
        bo_added = sem("bo_added")
        out_stored = sem("out_stored")
        att_tab = sem("att_tab")
        ident_ready = sem("ident_ready")
        a_loaded = sem("a_loaded")
        a_high = sem("a_high")
        a_low = sem("a_low")
        proj_ready = sem("proj_ready")
        rope_term = sem("rope_term")
        rope_taken = sem("rope_taken")
        rope_sum = sem("rope_sum")
        rope_high = sem("rope_high")
        rope_low = sem("rope_low")
        v_ready = sem("v_ready")
        v_high = sem("v_high")
        v_low = sem("v_low")
        v_loaded = [sem(f"v_loaded_{half}") for half in range(2)]
        s_ready = sem("s_ready")
        max_ready = sem("max_ready")
        exp_done = sem("exp_done")
        inv_ready = sem("inv_ready")
        p_by_act = sem("p_by_act")
        p_by_dve = sem("p_by_dve")
        pt_ready = sem("pt_ready")
        pt_high = sem("pt_high")
        pt_low = sem("pt_low")
        av_done = sem("av_done")
        ctx_high = sem("ctx_high")
        ctx_low = sem("ctx_low")
        out_ready = sem("out_ready")
        out_added = sem("out_added")
        misc_ready = sem("misc_ready")
        misc_high = sem("misc_high")
        misc_free = sem("misc_free")
        w1_loaded = sem("w1_loaded")
        w1_high = sem("w1_high")
        w1_split = sem("w1_split")
        rope_stored = [sem(f"rope_stored_{s}") for s in range(2)]
        v_stored = [sem(f"v_stored_{s}") for s in range(4)]
        qk_loaded = [sem(f"qk_loaded_{s}") for s in range(2)]

        class Phase:
            pass

        def phase(k):
            p = Phase()
            p.k, p.blocks, p.l1 = k, FFN_BLOCKS[k], FFN_BLOCKS[k] > 1
            p.g0, p.n0 = CHUNKS * sum(FFN_BLOCKS[:k]), sum(FFN_BLOCKS[:k])
            p.pre = k in PRE
            p.s0 = p.g0 + CHUNKS * sum(j in PRE for j in range(k + 1))
            p.entries = sum(j in PRE for j in range(k + 1))
            p.norms0 = p.s0 - (CHUNKS - 1) * p.entries
            p.tab = 1 if p.l1 else 0
            p.xb0 = CHUNKS * BLOCKS if k == 3 else 0
            p.last = "final" if k == 3 else "last"
            return p

        def walk(p, engine, step):
            def at(blk, c, par, kind):
                return p.g0 + CHUNKS * blk + c, p.s0 + CHUNKS * blk + c, c, blk, par, kind

            def block_steps(blk, par, kind, before):
                prev = None
                if before:
                    prev = at(blk - 1, CHUNKS - 1, 1 - par, before)
                step(at(blk, 0, par, kind), prev)
                with engine.Fori(1, CHUNKS) as c:
                    step(at(blk, c, par, kind), at(blk, c - 1, par, kind))

            par0, last = p.n0 % 2, p.blocks - 1
            block_steps(0, par0, p.last if last == 0 else "inner", None)
            if p.blocks > 1:
                with engine.Fori(0, (p.blocks - 2) // 2) as i:
                    block_steps(1 + 2 * i, 1 - par0, "inner", "inner")
                    block_steps(2 + 2 * i, par0, "inner", "inner")
                block_steps(last, (par0 + last) % 2, p.last, "inner")

        def tail(p):
            return (p.g0 + CHUNKS * p.blocks - 1, p.s0 + CHUNKS * p.blocks - 1, CHUNKS - 1,
                    p.blocks - 1, (p.n0 + p.blocks - 1) % 2, p.last)

        def positive(v):
            return not isinstance(v, int) or v > 0

        def wait(e, semaphore, v):
            if positive(v):
                e.wait_ge(semaphore, v)

        def wait_apart(e, *waits):
            for _, v in waits:
                if not isinstance(v, int):
                    e.compute_val(v)
            e.wait_ge(in_loaded, 16 * N_IN)
            for semaphore, v in waits:
                wait(e, semaphore, v)

        def pe_transpose_chunk(pe, s):
            pe.wait_ge(xn_ready, s + 1)
            wait(pe, aff_done, s)
            for k in range(KD):
                for t in range(TPC):
                    last = nc.tensor.transpose(ps[:, TPS + k, t * PART:(t + 1) * PART],
                                               xn[:, t, k * PART:(k + 1) * PART], ident[:])
            last.then_inc(tr_ready, 1)

        def pe_step(pe, p, at, prev):
            g, s, c, blk, par, kind = at
            pe.wait_ge(w_split, 4 * (p.n0 + blk + 1))
            pe.wait_ge(xT_ready, s - CHUNKS + 1)

            def mm1(j):
                wait(pe, gelu_done, HT * g + j + 1 - 4)
                first = True
                for wp, xp in PARTS:
                    for k in range(KD):
                        last = nc.tensor.matmul(
                            ps[:, HPS + j % 4, :],
                            w[par][:, wp, 0, k * HIDDEN + j * PART:k * HIDDEN + (j + 1) * PART],
                            xT[:, xp, k, bass.ds(c * CHUNK, CHUNK)], start=first,
                            stop=(wp, xp) == (0, 0) and k == KD - 1)
                        first = False
                last.then_inc(hid_ready, 1)

            for j in range(HT):
                mm1(j)
                if j >= LAG:
                    pe_second(pe, at, j - LAG)
                elif prev is not None:
                    pe_second(pe, prev, HT - LAG + j)
            if prev is not None and prev[5] != "final":
                pe_transpose_chunk(pe, prev[1])

        def pe_second(pe, at, j):
            g, s, c, blk, par, kind = at
            if j == 0:
                wait(pe, y_free, g)
            pe.wait_ge(low_done, HT * g + j + 1)
            for t in range(TPC):
                for n, (hp, wp) in enumerate(PARTS):
                    last = nc.tensor.matmul(
                        y_ps[:, t, :], hid[:, hp, j % 4, t * PART:(t + 1) * PART],
                        w[par][:, wp, 1, j * DIM:(j + 1) * DIM],
                        start=j == 0 and n == 0 and t % 2 == 0, stop=j == HT - 1 and n == 2,
                        skip_group_check=True)
            last.then_inc(mm2_done, 1)

        def pe_tail(pe, p):
            for j in range(HT - LAG, HT):
                pe_second(pe, tail(p), j)
            if p.last != "final":
                pe_transpose_chunk(pe, tail(p)[1])

        def act_affine(act, s, c, row):
            wait_apart(act, (tr_ready, s + 1),
                       (xT_ready, s))
            for k in range(KD):
                last = nc.scalar.activation(xTf[:, k, :], ps[:, TPS + k, :], ACT.Identity,
                                            bias=bT[:, bass.ds(row * KD + k, 1)],
                                            scale=gT[:, bass.ds(row * KD + k, 1)])
            last.then_inc(aff_done, 1)
            wait_apart(act, (aff_done, s + 1))
            nc.scalar.activation(xT[:, 0, :, bass.ds(c * CHUNK, CHUNK)], xTf[:], ACT.Copy)\
                .then_inc(xTh_done, 1)

        def act_step(act, p, at, prev):
            g, s, c, blk, par, kind = at

            def gelu(j):
                wait_apart(act, (hid_ready, HT * g + j + 1),
                           (low_done, HT * g + j + 1 - 4))
                nc.scalar.activation(gel[:, j % 4, :], ps[:, HPS + j % 4, :], ACT.Gelu,
                                     bias=b1[:, bass.ds((p.tab + blk) * HT + j, 1)]).then_inc(gelu_done, 1)

            def high(j):
                act.wait_ge(gelu_done, HT * g + j + 1)
                wait(act, mm2_done, HT * g + j + 1 - 4)
                nc.scalar.activation(hid[:, 0, j % 4, :], gel[:, j % 4, :], ACT.Copy).then_inc(round_done, 1)

            for j in range(HT + 1):
                if j < HT:
                    gelu(j)
                if j >= 1:
                    high(j - 1)
                if j == HT and prev is not None and prev[5] != "final":
                    act_affine(act, prev[1], prev[2], prev[3] + 1 if prev[5] == "inner" else 0)

        NORM_LINKS = 14

        def dve_take(dve, p, at):
            g, s, c, blk, par, kind = at
            tiles = bass.ds(c * TPC, TPC)
            dve.wait_ge(mm2_done, HT * g + HT)
            if p.l1:
                dve.wait_ge(xb_ready, p.xb0 + CHUNKS * blk + c + 1)
                add = xb[:, tiles, :]
            else:
                add = rows[:, B2_0:B2_0 + 1, :].broadcast_to([PART, TPC, DIM])
            nc.vector.tensor_tensor(rb[:], y_ps[:, :, :], add, ALU.add).then_inc(y_free, 1)
            dve.wait_ge(y_free, g + 1)
            if kind != "inner":
                nc.vector.scalar_tensor_tensor(x[:, tiles, :], rb[:], 0.5, x[:, tiles, :], ALU.mult, ALU.add)\
                    .then_inc(x_updated, 1)
                wait_apart(dve, (x_updated, CHUNKS * p.k + c + 1))

        def dve_norm(dve, s, c, inner, xb_made, before, chunks=1):
            n = [0]

            def link(ins):
                n[0] += 1
                ins.then_inc(dve_link, 1)
                links = before * NORM_LINKS
                if n[0] == 1:
                    wait_apart(dve, (dve_link, links + 1))
                else:
                    dve.wait_ge(dve_link, links + n[0])

            tiles = TPC * chunks

            def src(t):
                return rb[:, t, :] if inner else x[:, bass.ds(c * TPC + t, 1), :]

            def statistics():
                for t in range(tiles):
                    last = nc.vector.bn_stats(stats[:, t, :], src(t))
                link(last)

            def variance():
                for t in range(tiles):
                    last = nc.vector.bn_aggr(mv[:, t, :], stats[:, t, :])
                link(last)
                link(nc.vector.tensor_scalar(var[:, 0:tiles], mv[:, 0:tiles, 1], EPS, None, ALU.add))
                link(nc.vector.tensor_scalar(nt[:, 0:tiles].bitcast(i32), var[:, 0:tiles].bitcast(i32), 1, None,
                                             ALU.logical_shift_right))
                link(nc.vector.tensor_scalar(rstd[:, 0:tiles].bitcast(i32), nt[:, 0:tiles].bitcast(i32), -1.0,
                                             float(RSQRT_GUESS), ALU.mult, ALU.add))

            def newton():
                link(nc.vector.tensor_tensor(nt[:, 0:tiles], rstd[:, 0:tiles], rstd[:, 0:tiles], ALU.mult))
                link(nc.vector.scalar_tensor_tensor(nt[:, 0:tiles], nt[:, 0:tiles], -0.5, var[:, 0:tiles],
                                                    ALU.mult, ALU.mult))
                link(nc.vector.scalar_tensor_tensor(rstd[:, 0:tiles], nt[:, 0:tiles], 1.5, rstd[:, 0:tiles],
                                                    ALU.add, ALU.mult))

            def apply(chunk):
                assert n[0] == NORM_LINKS
                wait(dve, tr_ready, s + chunk)
                if not isinstance(xb_made, int) or xb_made > 0:
                    wait(dve, xb_ready, xb_made + chunk)
                for t in range(TPC):
                    at = chunk * TPC + t
                    last = nc.vector.tensor_scalar(xn[:, t, :], src(at), mv[:, at, 0:1], rstd[:, at:at + 1],
                                                   ALU.subtract, ALU.mult)
                last.then_inc(xn_ready, 1)

            return [statistics, variance, newton, newton, newton] + [lambda k=k: apply(k) for k in range(chunks)]

        def dve_low_input(dve, s, c):
            dve.wait_ge(xTh_done, s + 1)
            chunk = bass.ds(c * CHUNK, CHUNK)
            nc.vector.tensor_tensor(xT[:, 1, :, chunk], xTf[:], xT[:, 0, :, chunk].bitcast(f32),
                                    ALU.subtract).then_inc(xT_ready, 1)

        def dve_step(dve, p, at, prev):
            g, s, c, blk, par, kind = at

            def low(j):
                dve.wait_ge(round_done, HT * g + j + 1)
                nc.vector.tensor_tensor(hid[:, 1, j % 4, :], gel[:, j % 4, :],
                                        hid[:, 0, j % 4, :].bitcast(f32), ALU.subtract).then_inc(low_done, 1)

            parts = []
            if prev is not None and prev[5] != "final":
                parts = dve_norm(dve, prev[1], prev[2], prev[5] == "inner", xb_before(p, prev),
                                 prev[1] - (CHUNKS - 1) * p.entries)
            for j in range(HT):
                low(j)
                if j == 1 and prev is not None:
                    dve_take(dve, p, prev)
                if 2 <= j < 6:
                    for part in parts[:2 if j >= 4 else 1]:
                        part()
                    parts = parts[2 if j >= 4 else 1:]
            assert not parts
            if prev is not None and prev[5] != "final":
                dve_low_input(dve, prev[1], prev[2])

        def dve_entry(dve, p):
            if not p.pre:
                return
            s = p.s0 - CHUNKS
            parts = dve_norm(dve, s, 0, False, CHUNKS * BLOCKS if p.k == 3 else 0, p.norms0 - 1, CHUNKS)
            parts[0]()
            if p.k == 3:
                entry_low(dve, nc.vector, p, (0, 1))
            for part in parts[1:-CHUNKS]:
                part()
            for c in range(CHUNKS + 1):
                if c < CHUNKS:
                    parts[c - CHUNKS]()
                if c > 0:
                    dve_low_input(dve, s + c - 1, c - 1)

        def dve_tail(dve, p):
            g, s, c, blk, par, kind = tail(p)
            dve_take(dve, p, tail(p))
            if p.last != "final":
                for part in dve_norm(dve, s, c, False, xb_before(p, tail(p)), s - (CHUNKS - 1) * p.entries):
                    part()
                if p.k == 0:
                    dve_split_a0(dve)
                dve_low_input(dve, s, c)

        xb_flat = xb[:, :, :].rearrange("p t e -> p (t e)")
        xb_raw = xb_flat.rearrange("p (h n) -> p h n", h=2)

        def pool_xb(pool, s, c, blk, scaled):
            wait_apart(pool, (xn_ready, s + 1))
            tiles = bass.ds(c * TPC, TPC)

            def row(r):
                return rows[:, bass.ds(r, 1), :].broadcast_to([PART, TPC, DIM])

            if blk is None:
                nc.gpsimd.tensor_tensor(xb[:, tiles, :], xn[:], row(B2_1), ALU.add).then_inc(xb_ready, 1)
            else:
                nc.gpsimd.tensor_tensor(xb[:, tiles, :], xn[:], row(GAIN + blk), ALU.mult)\
                    .then_inc(xb_scaled, 1)
                wait_apart(pool, (xb_scaled, scaled + 1))
                nc.gpsimd.tensor_tensor(xb[:, tiles, :], xb[:, tiles, :], row(B2_1 + 1 + blk), ALU.add)\
                    .then_inc(xb_ready, 1)

        def quarter(buffer, q):
            return buffer[:, q // 2, q % 2 * HIDDEN:(q % 2 + 1) * HIDDEN]

        def entry_high(act, p):
            if p.pre:
                x_ready(act, p.k)
                act.wait_ge(w_loaded, 16 * (p.n0 + 1))
                for q in range(4):
                    nc.scalar.activation(quarter(w[p.n0 % 2][:, 0], q), quarter(xb_raw, q), ACT.Copy).then_inc(w_high, 1)

        def entry_low(e, engine, p, quarters):
            for q in quarters:
                e.wait_ge(w_high, 4 * p.n0 + q + 1)
                engine.tensor_tensor(quarter(w[p.n0 % 2][:, 1], q), quarter(xb_raw, q),
                                     quarter(w[p.n0 % 2][:, 0], q).bitcast(f32), ALU.subtract).then_inc(w_split, 1)

        def pool_split(pool, n, q, par):
            if q == 0:
                wait_apart(pool, (w_loaded, 16 * (n + 1)),
                           (mm2_done, (n - 1) * (HT * CHUNKS)))
            half, cols = q // 2, slice(q % 2 * HIDDEN, (q % 2 + 1) * HIDDEN)
            nc.gpsimd.tensor_copy(w[par][:, 0, half, cols], wraw[:, half, cols]).then_inc(w_high, 1)
            pool.wait_ge(w_high, n * 4 + q + 1)
            nc.gpsimd.tensor_tensor(w[par][:, 1, half, cols], wraw[:, half, cols],
                                    w[par][:, 0, half, cols].bitcast(f32), ALU.subtract).then_inc(w_split, 1)

        def pool_post(pool, p, at):
            g, s, c, blk, par, kind = at
            if p.k == 1:
                pool_xb(pool, s, c, None, None)
            elif p.l1 and kind == "inner":
                pool_xb(pool, s, c, blk, CHUNKS * blk + c + (CHUNKS * (BLOCKS - 1) if p.k == 3 else 0))

        def pool_step(pool, p, at, prev):
            g, s, c, blk, par, kind = at
            if prev is not None:
                pool_post(pool, p, prev)
            if kind == "inner" or p.k == 1:
                if isinstance(c, int):
                    pool_split(pool, p.n0 + blk + 1, 0, 1 - par)
                    pool_split(pool, p.n0 + blk + 1, 1, 1 - par)
                    pool_split(pool, p.n0 + blk + 1, 2, 1 - par)
                    pool_split(pool, p.n0 + blk + 1, 3, 1 - par)

        def xb_before(p, at):
            g, s, c, blk, par, kind = at
            if p.k == 0:
                return 0
            if p.k == 1:
                return c
            if p.k == 2:
                return CHUNKS + CHUNKS * blk + c if kind == "inner" else CHUNKS * BLOCKS
            return CHUNKS * BLOCKS + CHUNKS + CHUNKS * blk + c

        S_PS, AV_PS, MISC_PS = 0, 6, 7
        T_BANKS = (4, 5)

        ORDER = (
            dict(
                pe=("t1 m10- m11- t2 s0' s1' t3 o0- m0 m1 o1- s2' s3' m2 t4 t5 m3 o2- s4' t6 "
                   "t7 m4 m5 o3- t8 t9 s5' m6 m7 t10 t11 m8 s6' t0' s7' m9"),
                act=("high5- c0- exp2 high6- high7- exp3 high8- high9- high10- exp4 high11- "
                   "exp5 high0 exp6 high1 c1- exp7 high2 n6 n7 high3 exp0' exp1' high4"),
                dve=("inv5 max7 low0 inv6 low1 c1- n4 inv7 o0- max0' low2 n5 max1' max2' low3 "
                   "o1- max3' inv0' inv1' low4 low5 c0 n0' inv2' o2- low6 low7 o3- n1' max4' "
                   "low8 low9 inv3' n2' max5' n3' low10 inv4' max6' low11"),
            ),
            dict(
                pe=("s6 wo3- s7 k0' m0 t2 t3 k1' v0' v1' q0' m1 m2 m3 t4 t5 q1' m4 t6 t7 m5 "
                   "s0' s1' wo0 t8 m6 t9 wo1 t10 m7 s2' t11 w0' s3' m8 m9 m10 m11 s4' w1' "
                   "s5' t0' t1' wo2"),
                act=("high10- w0 high11- exp2 exp3 c1- w1 exp4 high0 exp5 high1 k0' exp6 high2 "
                   "k1' high3 exp7 q0' c0 high4 high5 q1' high6 high7 exp0' high8 high9 "
                   "exp1'"),
                dve=("q1 low6- inv4- inv5- max0 low7- wo0- low8- max1 low9- wo1- low10- inv6- "
                   "max2 max3 low11- w0 max4 c1- inv7- w1 max5 wo2- low0 max6 wo3- low1 k0' "
                   "k1' max7 v0' low2 low3 inv0 v1' inv1 inv2 q0' inv3 c0 low4 low5"),
            ),
        )

        BY_ACT = [int(word[1]) for word in ORDER[0]["act"].split() if word[0] == "n"]
        BY_DVE = [qt for qt in range(QT) if qt not in BY_ACT]

        def in_order(kind, engine, heads, first=0, last=GROUP):
            todo = []
            for h in heads:
                for word in ORDER[kind][engine].split():
                    item = word.strip("'-0123456789")
                    head = h + word.count("'") - word.count("-")
                    of_group = {"o": GROUP - 1, "k": 0, "v": 0, "w": 0}.get(item, head % GROUP)
                    if first <= head < last and head % GROUP == of_group:
                        todo.append((item, head, int(word[len(item):].strip("'-"))))
            return todo

        def count_in(engine, items, per_group):
            order = [item for item in in_order(1, engine, range(-1, 3 * GROUP + 1), 0, 3 * GROUP) if item[0] in items]
            counts = [{(item, h - group * GROUP, k): n - group * per_group
                       for n, (item, h, k) in enumerate(order) if h // GROUP == group} for group in range(3)]
            assert all(len(count) == per_group for count in counts)
            return counts

        def which_group(i1):
            return 1 if not isinstance(i1, int) or 0 < i1 < GROUPS - 1 else 2 * (i1 > 0)

        USES = count_in("pe", ("k", "v", "w", "q", "wo"), A1_MISC)
        HIGHS = count_in("act", ("k", "w", "q"), A1_HIGHS)
        assert USES == count_in("dve", ("k", "v", "w", "q", "wo"), A1_MISC)

        def uses(i1, item, h, n):
            group = i1 + h // GROUP
            return A1_MISC * group + USES[which_group(group)][item, h % GROUP, n]

        def score_banks(qt):
            return (S_PS + qt, 1) if qt < 4 else (S_PS + 2 * (qt % 2), 2)

        def score_view(qt):
            bank, n = score_banks(qt)
            return ps[:, bank:bank + n, :].rearrange("p b n -> p (b n)")[:, 0:(qt + 1) * PART]

        BANK_USED = {0: -1, 1: -1, 2: 0, 3: 0, 4: 2, 5: 4, 6: 5, 7: 6}

        def key_tile(m):
            qc, kt = (0, m) if m < 4 else (1, m - 4)
            return qc, kt, max(0, kt - 4 * qc)

        def attention(e, kind, engine, items):
            def run(i1, *span):
                group = [items(e, kind, i1 + over) for over in (-1, 0, 1)]
                for item, head, n in in_order(kind, engine, *span):
                    group[head // GROUP + 1][item](head % GROUP, n)

            run(0, range(-1, GROUP), 0, 2 * GROUP)
            with e.Fori(1, GROUPS - 1) as i1:
                run(i1, range(GROUP), -1, 2 * GROUP)
            run(GROUPS - 1, range(GROUP + 1), -1, GROUP)

        def group_of(kind, i1):
            return i1 + GROUPS * kind, i1 // (GROUPS // BATCH), i1 % (GROUPS // BATCH)

        def a1_piece(part, which, h=0, k=0):
            at = {"k": 0, "v": 1, "q": 2 + h, "o": 6 + h}[which] * DIM
            if which == "o":
                return w_a1[:, part, at:at + DIM]
            return w_a1[:, part, at + k * HD1:at + (k + 1) * HD1]

        A1_PIECE = {"k": 0, "v": 1, "q": 2, "o": 6}

        def pe_att(pe, kind, i1):
            i, b, g = group_of(kind, i1)

            def scores(h, qt):
                u, width = GROUP * i + h, (qt + 1) * PART
                wait(pe, exp_done, QT * u + BANK_USED[qt])
                if qt == 0:
                    if kind:
                        pe.wait_ge(misc_free, uses(i1, "q", h, 1) + 1)
                    else:
                        pe.wait_ge(qk_loaded[h % 2], 128 * (2 * i + h // 2 + 1))
                base = score_banks(qt)[0]
                for bank in range((width + CHUNK - 1) // CHUNK):
                    n = min(CHUNK, width - bank * CHUNK)
                    dst = ps[:, base + bank, 0:n]
                    q, k = slice(qt * PART, (qt + 1) * PART), slice(bank * CHUNK, bank * CHUNK + n)
                    diagonal = bank == qt // 4
                    if kind:
                        for x3, (qp, kp) in enumerate(PARTS):
                            last = nc.tensor.matmul(dst, q_sb[:, h % 2, qp, q], k_sb[:, kp, k],
                                                    start=x3 == 0, stop=x3 == 2 and not diagonal)
                    else:
                        last = nc.tensor.matmul(dst, q_st[:, h % 2, q], k_st[:, h % 2, k],
                                                start=True, stop=not diagonal)
                    if diagonal:
                        last = nc.tensor.matmul(ps[:, base + bank, n - PART:n], ident_b[:], mask_b[:],
                                                start=False, stop=True)
                last.then_inc(s_ready, 1)

            def transpose(h, m):
                u, (qc, kt, q0) = GROUP * i + h, key_tile(m)
                if kt == 0:
                    if kind:
                        pe.wait_ge(exp_done, QT * u + 4 * qc + 4)
                    else:
                        for done, mine in ((p_by_act, BY_ACT), (p_by_dve, BY_DVE)):
                            pe.wait_ge(done, len(mine) * u + sum(qt < 4 * qc + 4 for qt in mine))
                wait(pe, pt_low, 12 * u + m - 1)
                p = p_hi if qc else p_lo
                for qi in range(q0, TPC):
                    last = nc.tensor.transpose(ps[:, T_BANKS[m % 2], qi * PART:(qi + 1) * PART],
                                               p[:, qi, kt * PART:(kt + 1) * PART], ident[:])
                last.then_inc(pt_ready, 1)

            def product(h, m):
                u, (qc, kt, q0) = GROUP * i + h, key_tile(m)
                if h == 0 and m in (0, 8):
                    if kind:
                        pe.wait_ge(misc_free, uses(i1, "w", 0, m // 8) + 1)
                    else:
                        pe.wait_ge(v_loaded[m // 8], 16 * (i + 1))
                pe.wait_ge(pt_low, 12 * u + m + 1)
                if kt == 0:
                    wait(pe, ctx_low, 2 * u + qc)
                cols = slice(q0 * PART, CHUNK)
                passes = ([(v_sb[:, vp, kt, :], pp) for vp, pp in PARTS] if kind
                          else [(v_st[:, kt, :], 1), (v_st[:, kt, :], 0)])
                for n, (v, pp) in enumerate(passes):
                    last = nc.tensor.matmul(ps[:, AV_PS, cols], v, pT[:, pp, m % PT_SLOTS, cols],
                                            start=kt == 0 and n == 0,
                                            stop=kt == 3 + 4 * qc and n == len(passes) - 1)
                last.then_inc(av_done, 1)

            def project(which, h, half):
                pe.wait_ge(w1_split, 10 * i1 + A1_PIECE[which] + h + 1)
                wait(pe, misc_free, uses(i1, which, h, half))
                first = True
                for wp, xp in PARTS:
                    for k in range(KD):
                        last = nc.tensor.matmul(ps[:, MISC_PS, :], a1_piece(wp, which, h, k),
                                                xT[:, xp, k, bass.ds(b * SEQ + half * CHUNK, CHUNK)],
                                                start=first, stop=(wp, xp) == (0, 0) and k == KD - 1)
                        first = False
                last.then_inc(misc_ready, 1)

            def transpose_values(h, r):
                wait(pe, misc_free, uses(i1, "w", h, r))
                for t in range(TPC):
                    last = nc.tensor.transpose(ps[:, MISC_PS, t * PART:(t + 1) * PART],
                                               xTf[:, r, t * PART:(t + 1) * PART], ident[:])
                last.then_inc(misc_ready, 1)

            def out_tiles(t0, weight, done):
                for t in range(2):
                    for n, (cp, wp) in enumerate(PARTS):
                        last = nc.tensor.matmul(ps[:, MISC_PS, t * DIM:(t + 1) * DIM],
                                                ctxT[:, cp, (t0 + t) * PART:(t0 + t + 1) * PART], weight(wp),
                                                start=t == 0 and n == 0, stop=n == 2, skip_group_check=True)
                last.then_inc(done, 1)

            def head_output(h, r):
                pe.wait_ge(ctx_low, 2 * (GROUP * i + h) + r // 2 + 1)
                pe.wait_ge(misc_free, uses(i1, "wo", h, r))
                pe.wait_ge(w1_split, 10 * i1 + 6 + h + 1)
                out_tiles(2 * r, lambda wp: a1_piece(wp, "o", h), misc_ready)

            def group_output(h, r):
                pe.wait_ge(ctx_low, 2 * (GROUP * i + h) + r // 2 + 1)
                wait(pe, out_added, 4 * i + r)
                out_tiles(2 * r, lambda wp: w_a0[:, wp, bass.ds(g * DIM + 5 * KD * DIM, DIM)], out_ready)

            return dict(s=scores, t=transpose, m=product, o=group_output, wo=head_output, w=transpose_values,
                        q=lambda h, half: project("q", h, half), k=lambda h, half: project("k", h, half),
                        v=lambda h, half: project("v", h, half))

        def act_att(act, kind, i1):
            i, b, g = group_of(kind, i1)

            def exp(h, qt):
                u = GROUP * i + h
                act.wait_ge(max_ready, QT * u + qt + 1)
                wait(act, pt_ready, 12 * (u - 1) + (12 if qt >= 4 else 4))
                p = p_hi if qt >= 4 else p_lo
                nc.scalar.activation(p[:, qt % 4, 0:(qt + 1) * PART], score_view(qt), ACT.Exp,
                                     bias=negmax[:, h % 2, qt:qt + 1],
                                     accum_out=rowsum[:, h % 2, qt:qt + 1]).then_inc(exp_done, 1)

            def high(h, m):
                u, q0 = GROUP * i + h, key_tile(m)[2]
                act.wait_ge(pt_ready, 12 * u + m + 1)
                wait(act, av_done, 12 * u + m + 1 - PT_SLOTS)
                nc.scalar.activation(pT[:, 0, m % PT_SLOTS, q0 * PART:],
                                     ps[:, T_BANKS[m % 2], q0 * PART:],
                                     ACT.Copy).then_inc(pt_high, 1)

            def ctx_part(h, qc):
                u, cols = GROUP * i + h, slice(qc * CHUNK, (qc + 1) * CHUNK)
                act.wait_ge(av_done, 12 * u + 4 + 8 * qc)
                if kind:
                    wait(act, misc_ready, uses(i1, "wo", h - 1, 2 * qc + 1) + 1)
                elif h == 0:
                    wait(act, out_ready, 4 * i - 2 + 2 * qc)
                mine = slice(0, PART) if kind else slice(32 * h, 32 * h + 32)
                nc.scalar.activation(ctxT[mine, 0, cols], ps[mine, AV_PS, :], ACT.Copy).then_inc(ctx_high, 1)

            def normalise(h, qt):
                act.wait_ge(inv_ready, QT * (GROUP * i + h) + qt + 1)
                p = (p_hi if qt >= 4 else p_lo)[:, qt % 4, 0:(qt + 1) * PART]
                nc.scalar.activation(p, p, ACT.Copy, scale=rowinv[:, h % 2, qt:qt + 1]).then_inc(p_by_act, 1)

            def projected(which, h, half):
                act.wait_ge(misc_ready, uses(i1, which, h, half) + 1)
                if which == "w":
                    wait(act, av_done, 12 * GROUP * i - 4 * (1 - half))
                    dst = v_sb[:, 0, 4 * half:4 * half + 4, :].rearrange("p t n -> p (t n)")
                else:
                    wait(act, s_ready, QT * (GROUP * i + h - (which == "q")))
                    dst = (k_sb if which == "k" else q_sb[:, h % 2])[:, 0, half * CHUNK:(half + 1) * CHUNK]
                nc.scalar.activation(dst, ps[:, MISC_PS, :], ACT.Copy).then_inc(misc_high, 1)

            return dict(exp=exp, high=high, c=ctx_part, n=normalise,
                        q=lambda h, half: projected("q", h, half), k=lambda h, half: projected("k", h, half),
                        w=lambda h, half: projected("w", h, half))

        def dve_att(dve, kind, i1):
            i, b, g = group_of(kind, i1)

            def maximum(h, qt):
                dve.wait_ge(s_ready, QT * (GROUP * i + h) + qt + 1)
                nc.vector.tensor_reduce(negmax[:, h % 2, qt:qt + 1], score_view(qt), AX.X, ALU.max,
                                        negate=True).then_inc(max_ready, 1)

            def inverse(h, qt):
                dve.wait_ge(exp_done, QT * (GROUP * i + h) + qt + 1)
                nc.vector.reciprocal(rowinv[:, h % 2, qt:qt + 1], rowsum[:, h % 2, qt:qt + 1])\
                    .then_inc(inv_ready, 1)

            def low(h, m):
                q0 = key_tile(m)[2]
                dve.wait_ge(pt_high, 12 * (GROUP * i + h) + m + 1)
                nc.vector.tensor_tensor(pT[:, 1, m % PT_SLOTS, q0 * PART:],
                                        ps[:, T_BANKS[m % 2], q0 * PART:],
                                        pT[:, 0, m % PT_SLOTS, q0 * PART:].bitcast(f32),
                                        ALU.subtract).then_inc(pt_low, 1)

            def ctx_part(h, qc):
                u, cols = GROUP * i + h, slice(qc * CHUNK, (qc + 1) * CHUNK)
                mine = slice(0, PART) if kind else slice(32 * h, 32 * h + 32)
                dve.wait_ge(ctx_high, 2 * u + qc + 1)
                nc.vector.tensor_tensor(ctxT[mine, 1, cols], ps[mine, AV_PS, :],
                                        ctxT[mine, 0, cols].bitcast(f32), ALU.subtract).then_inc(ctx_low, 1)

            def normalise(h, qt):
                dve.wait_ge(inv_ready, QT * (GROUP * i + h) + qt + 1)
                p = (p_hi if qt >= 4 else p_lo)[:, qt % 4, 0:(qt + 1) * PART]
                nc.vector.tensor_scalar(p, p, rowinv[:, h % 2, qt:qt + 1], None, ALU.mult).then_inc(p_by_dve, 1)

            def projected(which, h, half):
                dve.wait_ge(misc_high, A1_HIGHS * i1 + HIGHS[which_group(i1)][which, h, half] + 1)
                cols = slice(half * CHUNK, (half + 1) * CHUNK)
                whole, rest = (v_sb[:, part, 4 * half:4 * half + 4, :].rearrange("p t n -> p (t n)") if which == "w"
                               else (k_sb if which == "k" else q_sb[:, h % 2])[:, part, cols] for part in (0, 1))
                nc.vector.tensor_tensor(rest, ps[:, MISC_PS, :], whole.bitcast(f32), ALU.subtract)\
                    .then_inc(misc_free, 1)

            def take_values(h, half):
                dve.wait_ge(misc_ready, uses(i1, "v", h, half) + 1)
                nc.vector.tensor_copy(xTf[:, half, :], ps[:, MISC_PS, :]).then_inc(misc_free, 1)

            def add_head(h, r):
                dve.wait_ge(misc_ready, uses(i1, "wo", h, r) + 1)
                dve.wait_ge(inv_ready, QT * (GROUP * i + h) + 2 * r + 2)
                if h == 0 and r == 0:
                    dve.wait_ge(bo_added, CHUNKS)
                for t in range(2):
                    dst = x[:, bass.ds(b * QT + 2 * r + t, 1), :].rearrange("p o e -> p (o e)")
                    last = nc.vector.scalar_tensor_tensor(dst, ps[:, MISC_PS, t * DIM:(t + 1) * DIM],
                                                          rowinv[:, h % 2, 2 * r + t:2 * r + t + 1], dst,
                                                          ALU.mult, ALU.add)
                last.then_inc(misc_free, 1)

            def add_group(h, r):
                dve.wait_ge(out_ready, 4 * i + r + 1)
                dst = x[:, bass.ds(b * QT + 2 * r, 2), :]
                nc.vector.tensor_tensor(dst, ps[:, MISC_PS, :].rearrange("p (t e) -> p t e", t=2), dst,
                                        ALU.add).then_inc(out_added, 1)

            return dict(max=maximum, inv=inverse, low=low, c=ctx_part, n=normalise, v=take_values, wo=add_head,
                        o=add_group, q=lambda h, half: projected("q", h, half),
                        k=lambda h, half: projected("k", h, half), w=lambda h, half: projected("w", h, half))

        def last_use(piece):
            return max(n + 1 for uses_ in USES for (which, h, _), n in uses_.items()
                       if which != "w" and piece == A1_PIECE["o" if which == "wo" else which] + h)

        def pool_split_a1(pool, i, first):
            wait_apart(pool, (w1_loaded, 16 * (i + 1)))
            for piece in range(10):
                cols = slice(piece * DIM, (piece + 1) * DIM)
                if not first:
                    wait_apart(pool, (misc_ready, A1_MISC * (i - 1) + last_use(piece)))
                nc.gpsimd.tensor_copy(w_a1[:, 0, cols], xb[:, piece, :]).then_inc(w1_high, 1)
                pool.wait_ge(w1_high, 10 * i + piece + 1)
                nc.gpsimd.tensor_tensor(w_a1[:, 1, cols], xb[:, piece, :], w_a1[:, 0, cols].bitcast(f32),
                                        ALU.subtract).then_inc(w1_split, 1)

        PIECES = [(qk, half) for qk in range(2) for half in range(KD)]
        V_W = 4 * KD * DIM

        def a0_raw(piece):
            return (slice(V_W, A0_W), slice(0, 2 * KD * DIM), slice(2 * KD * DIM, V_W))[piece]

        def rope_pieces(e, body):
            for n in range(2 * BATCH * len(PIECES)):
                chunk, (qk, half) = n // len(PIECES), PIECES[n % len(PIECES)]
                body(n, chunk * CHUNK, chunk * CHUNK % SEQ, qk, half, n % 2)

        def pe_project_a0(pe):
            pe.wait_ge(xT_ready, S_ATT[0])

            def piece(n, token, seq, qk, half, slot):
                if n >= 2:
                    pe.wait_ge(rope_taken, n - 1)
                for swap in range(2):
                    pe.wait_ge(a_low, qk + 2)
                    first = True
                    for wp, xp in PARTS:
                        for k in range(KD):
                            at = ((2 * qk + swap) * KD + k) * DIM + half * PART
                            last = nc.tensor.matmul(ps[:, 2 * slot + swap, :], w_a0[:, wp, at:at + PART],
                                                    xT[:, xp, k, bass.ds(token, CHUNK)], start=first,
                                                    stop=(wp, xp) == (0, 0) and k == KD - 1)
                            first = False
                last.then_inc(proj_ready, 1)

            pe.wait_ge(a_low, 1)
            for t in range(TILES):
                wait(pe, v_low, t - 3)
                first = True
                for wp, xp in PARTS:
                    for k in range(KD):
                        last = nc.tensor.matmul(ps[:, 4 + t % 4, 0:DIM],
                                                xT[:, xp, k, t * PART:(t + 1) * PART],
                                                w_a0[:, wp, V_W + k * DIM:V_W + (k + 1) * DIM], start=first,
                                                stop=(wp, xp) == (0, 0) and k == KD - 1)
                        first = False
                last.then_inc(v_ready, 1)
            rope_pieces(pe, piece)
            pe.wait_ge(v_low, TILES)
            pe.wait_ge(rope_taken, 2 * BATCH * len(PIECES))

        def act_split_a0(act):
            act.wait_ge(a_loaded, 16)
            act.wait_ge(mm2_done, HT * CHUNKS)
            for piece in range(3):
                nc.scalar.activation(w_a0[:, 0, a0_raw(piece)], xb_flat[:, a0_raw(piece)], ACT.Copy)\
                    .then_inc(a_high, 1)

        def dve_split_a0(dve):
            for piece in range(3):
                dve.wait_ge(a_high, piece + 1)
                nc.vector.tensor_tensor(w_a0[:, 1, a0_raw(piece)], xb_flat[:, a0_raw(piece)],
                                        w_a0[:, 0, a0_raw(piece)].bitcast(f32), ALU.subtract)\
                    .then_inc(a_low, 1)

        def act_project_a0(act):
            def piece(n, token, seq, qk, half, slot):
                act.wait_ge(rope_sum, n + 1)
                if n >= 2:
                    act.wait_ge(rope_stored[slot], 16 * (n // 2))
                nc.scalar.activation(rope_hl[:, 0, slot, :], rope[:, 2, slot, :], ACT.Copy)\
                    .then_inc(rope_high, 1)
            for t in range(TILES):
                act.wait_ge(v_ready, t + 1)
                wait(act, v_stored[t % 4], 16 * (t // 4))
                nc.scalar.activation(v_hl[:, t % 4, :, 0, :],
                                     ps[:, 4 + t % 4, 0:DIM].rearrange("p (h d) -> p h d", h=HEADS),
                                     ACT.Copy).then_inc(v_high, 1)
            rope_pieces(act, piece)

        def dve_project_a0(dve):
            def low_part(n):
                dve.wait_ge(rope_high, n + 1)
                nc.vector.tensor_tensor(rope_hl[:, 1, n % 2, :], rope[:, 2, n % 2, :],
                                        rope_hl[:, 0, n % 2, :].bitcast(f32), ALU.subtract).then_inc(rope_low, 1)

            def piece(n, token, seq, qk, half, slot):
                dve.wait_ge(proj_ready, n + 1)
                for term in range(2):
                    nc.vector.tensor_tensor(rope[:, term, slot, :], ps[:, 2 * slot + term, :],
                                            rot[:, 2 * qk + term, seq:seq + CHUNK], ALU.mult)\
                        .then_inc(rope_taken if term else rope_term, 1)
                if n:
                    low_part(n - 1)
                dve.wait_ge(rope_taken, n + 1)
                nc.vector.tensor_tensor(rope[:, 2, slot, :], rope[:, 0, slot, :], rope[:, 1, slot, :],
                                        ALU.add).then_inc(rope_sum, 1)

            for t in range(TILES):
                dve.wait_ge(v_high, t + 1)
                nc.vector.tensor_tensor(v_hl[:, t % 4, :, 1, :],
                                        ps[:, 4 + t % 4, 0:DIM].rearrange("p (h d) -> p h d", h=HEADS),
                                        v_hl[:, t % 4, :, 0, :].bitcast(f32), ALU.subtract)\
                    .then_inc(v_low, 1)
            dve.wait_ge(att_tab, 16)
            rope_pieces(dve, piece)
            low_part(2 * BATCH * len(PIECES) - 1)

        def sp_project_a0(sp, load):
            def piece(n, token, seq, qk, half, slot):
                if n == BATCH * len(PIECES):
                    for stored in rope_stored:
                        sp.wait_ge(stored, 16 * len(PIECES))
                sp.wait_ge(rope_low, n + 1)
                sp.dma_start(qk_dram[qk, half * PART:(half + 1) * PART, :, bass.ds(token, CHUNK)],
                             rope_hl[:, :, slot, :].bitcast(f32)).then_inc(rope_stored[slot], 16)
                if n >= BATCH * len(PIECES):
                    h, row = divmod(n - BATCH * len(PIECES), 4)
                    load_row(h, 0, 0, row)

            def load_row(h, b, g, row):
                for dst, qk, part in ((q_st, 0, row % 2), (k_st, 1, row // 2)):
                    sp.dma_start(dst[row * HD0:(row + 1) * HD0, h % 2, :].bitcast(f32),
                                 qk_dram[qk, bass.ds((GROUP * g + h) * HD0, HD0), part,
                                         bass.ds(b * SEQ, SEQ)]).then_inc(qk_loaded[h % 2], 16)

            def load_values(half, b, g):
                sp.dma_start(v_st[:, 4 * half:4 * half + 4, :].bitcast(f32),
                             v_dram[bass.ds(b * QT + 4 * half, 4), :, bass.ds(g * PART, PART)]
                             .rearrange("t p n -> p t n")).then_inc(v_loaded[half], 16)

            for t in range(TILES):
                sp.wait_ge(v_low, t + 1)
                sp.dma_start(v_dram[t, :, :],
                             v_hl[:, t % 4, :, :, :].rearrange("p h a d -> p (h a d)").bitcast(f32))\
                    .then_inc(v_stored[t % 4], 16)
            rope_pieces(sp, piece)
            for stored in v_stored:
                sp.wait_ge(stored, 16 * TILES // 4)
            for half in range(2):
                load_values(half, 0, 0)
            sp.wait_ge(a_low, 3)
            load(1, 0, xb_raw)
            for stored in rope_stored:
                sp.wait_ge(stored, 16 * 2 * len(PIECES))

            def group(i, b, g, first=0):
                for h in range(first, GROUP):
                    if h >= 2 or not first:
                        wait_apart(sp, (s_ready, QT * (GROUP * i + h - 1)))
                    for row in range(4):
                        load_row(h, b, g, row)
                    if h == 1:
                        for half in range(2):
                            wait_apart(sp, (av_done, 12 * GROUP * i - 4 * (1 - half)))
                            load_values(half, b, g)

            group(0, 0, 0, first=2)
            for b in range(BATCH):
                with sp.Fori(1 - b, GROUPS // BATCH) as g:
                    group(b * (GROUPS // BATCH) + g, b, g)

        ATT_END = {0: (out_added, 4 * GROUPS), 1: (misc_free, A1_MISC * GROUPS)}
        S_ATT = {0: CHUNKS * 2, 1: CHUNKS * (2 + 1 + 1 + BLOCKS)}
        ATT_BEFORE = {1: 0, 3: 1}

        def x_ready(e, k):
            if k == 0:
                e.wait_ge(in_loaded, 16 * N_IN)
                e.wait_ge(tab_ready, 1)
                return
            e.wait_ge(*ATT_END[ATT_BEFORE[k]])
            if k == 3:
                e.wait_ge(bo_added, CHUNKS)

        def pre_posts(e, k, body):
            p = phase(k)
            if p.pre:
                for c in range(CHUNKS):
                    body(p, p.s0 - CHUNKS + c, c)

        N_IN = 9

        block = ctx.enter_context(nc.Block())

        @block.sync
        def _(sp):
            for t in range(CHUNKS):
                tiles = slice(t * TPC, (t + 1) * TPC)
                sp.dma_start(x[:, tiles, :], a["x"].rearrange("(t p) e -> p t e", p=PART)[:, tiles, :])\
                    .then_inc(in_loaded, 16)
            sp.dma_start(ident[:], a["ident"]).then_inc(in_loaded, 16)
            sp.dma_start(b1[:], a["b1"]).then_inc(in_loaded, 16)
            sp.dma_start(gT[:, KD:], a["gT"]).then_inc(in_loaded, 16)
            sp.dma_start(bT[:, KD:], a["bT"]).then_inc(in_loaded, 16)
            sp.dma_start(rows[:], a["rows"].partition_broadcast(PART)).then_inc(in_loaded, 16)
            sp.dma_start(lnb[:], a["lnb"].partition_broadcast(PART)).then_inc(lnb_loaded, 16)
            sp.dma_start(rb[:, 0, 0:PART], a["mask"]).then_inc(lnb_loaded, 16)

            def load(n, source, raw=wraw):
                if positive(n):
                    wait_apart(sp, (w_split, 4 * n))
                sp.dma_start(raw[:], a["wffn"][bass.ds(source, 1), :, :].rearrange(
                    "o p (h n) -> p (o h) n", h=2)).then_inc(w_loaded, 16)

            for k in range(PHASES):
                p = phase(k)
                if k == 0:
                    load(0, 0, xb_raw)
                    sp.dma_start(rot[:], a["rot"]).then_inc(att_tab, 16)
                    sp.wait_ge(w_split, 4)
                    sp.dma_start(xb_flat[:, 0:A0_W], a["w_a0"]).then_inc(a_loaded, 16)
                if k == 1:
                    sp_project_a0(sp, load)
                if k == 3:
                    sp.wait_ge(xT_ready, S_ATT[1])
                    sp.dma_start(xb[:, 0:10, :], a["w_a1"][0, :, :].rearrange("p (t e) -> p t e", e=DIM))\
                        .then_inc(w1_loaded, 16)
                    with sp.Fori(1, GROUPS) as i:
                        wait_apart(sp, (w1_split, 10 * i))
                        sp.dma_start(xb[:, 0:10, :], a["w_a1"][bass.ds(i, 1), :, :].rearrange(
                            "o p (t e) -> p (o t) e", e=DIM)).then_inc(w1_loaded, 16)
                if k == 3:
                    sp.wait_ge(w1_split, 10 * GROUPS)
                    load(p.n0, p.tab, xb_raw)
                if k == 1:
                    load(p.n0 + 1, 1)
                if p.l1:
                    with sp.Fori(1, p.blocks) as blk:
                        load(p.n0 + blk, p.tab + blk)
            for c in range(CHUNKS):
                sp.wait_ge(x_updated, CHUNKS * (PHASES - 1) + c + 1)
                sp.dma_start(a["out"].rearrange("(t p) e -> p t e", p=PART)[:, c * TPC:(c + 1) * TPC, :],
                             x[:, c * TPC:(c + 1) * TPC, :]).then_inc(out_stored, 16)
            sp.wait_ge(out_stored, 16 * CHUNKS)

        @block.gpsimd
        def _(pool):
            nc.gpsimd.memset(gT[:, 0:KD], 1.0)
            nc.gpsimd.memset(bT[:, 0:KD], 0.0).then_inc(tab_ready, 1)
            pool.wait_ge(in_loaded, 16 * N_IN)
            pool.wait_ge(lnb_loaded, 32)
            nc.gpsimd.tensor_copy(ident_b[:], ident[:]).then_inc(ident_ready, 1)
            nc.gpsimd.tensor_copy(mask_b[:], rb[:, 0, 0:PART]).then_inc(ident_ready, 1)
            nc.gpsimd.tensor_tensor(rows[:, B2_1 + 1:B2_1 + BLOCKS, :], rows[:, B2_1 + 1:B2_1 + BLOCKS, :],
                                    lnb[:], ALU.add).then_inc(rows_ready, 1)
            pool.wait_ge(rows_ready, 1)
            for k in range(PHASES):
                p = phase(k)
                if k == 3:
                    pool.wait_ge(xn_ready, S_ATT[1])
                    for c in range(CHUNKS):
                        tiles = slice(c * TPC, (c + 1) * TPC)
                        nc.gpsimd.tensor_tensor(x[:, tiles, :], x[:, tiles, :], rows[:, BO:BO + 1, :]
                                                .broadcast_to([PART, TPC, DIM]), ALU.add).then_inc(bo_added, 1)
                if k == 3:
                    pool_split_a1(pool, 0, True)
                    with pool.Fori(1, GROUPS) as i:
                        pool_split_a1(pool, i, False)
                if p.pre:
                    entry_low(pool, nc.gpsimd, p, (2, 3) if k == 3 else range(4))
                if k == 3:
                    pool.wait_ge(w_split, 4 * (p.n0 + 1))
                    pre_posts(pool, k, lambda p, s, c: pool_xb(pool, s, c, None, None))
                walk(p, pool, lambda at, prev: pool_step(pool, p, at, prev))
                pool_post(pool, p, tail(p))

        @block.scalar
        def _(act):
            act.wait_ge(in_loaded, 16 * N_IN)
            act.wait_ge(tab_ready, 1)
            for k in range(PHASES):
                p = phase(k)
                if k == 1:
                    act_project_a0(act)
                    for stored in v_stored:
                        act.wait_ge(stored, 16 * TILES // 4)
                    for stored in rope_stored:
                        act.wait_ge(stored, 16 * 2 * len(PIECES))
                    attention(act, 0, "act", act_att)
                if k == 3:
                    act.wait_ge(xT_ready, S_ATT[1])
                    attention(act, 1, "act", act_att)
                entry_high(act, p)
                pre_posts(act, k, lambda p, s, c: act_affine(act, s, c, 0))
                walk(p, act, lambda at, prev: act_step(act, p, at, prev))
                if k == 0:
                    act_split_a0(act)
                if p.last != "final":
                    act_affine(act, tail(p)[1], CHUNKS - 1, 0)

        @block.vector
        def _(dve):
            dve.wait_ge(ident_ready, 2)
            for k in range(PHASES):
                p = phase(k)
                if k == 1:
                    dve_project_a0(dve)
                    attention(dve, 0, "dve", dve_att)
                if k == 3:
                    attention(dve, 1, "dve", dve_att)
                if p.pre:
                    x_ready(dve, k)
                dve_entry(dve, p)
                walk(p, dve, lambda at, prev: dve_step(dve, p, at, prev))
                dve_tail(dve, p)

        @block.tensor
        def _(pe):
            pe.wait_ge(in_loaded, 16 * N_IN)
            for k in range(PHASES):
                p = phase(k)
                if k == 1:
                    pe.wait_ge(ident_ready, 2)
                    pe_project_a0(pe)
                    attention(pe, 0, "pe", pe_att)
                if k == 3:
                    pe.wait_ge(xT_ready, S_ATT[1])
                    attention(pe, 1, "pe", pe_att)
                pre_posts(pe, k, lambda p, s, c: pe_transpose_chunk(pe, s))
                walk(p, pe, lambda at, prev: pe_step(pe, p, at, prev))
                pe_tail(pe, p)


def rotation():
    f = np.float32
    inverse = (f(1) / np.power(f(ROPE_BASE), np.arange(0, HD0, 2, dtype=f) / f(HD0))).astype(f)
    angles = np.outer(inverse, np.arange(SEQ, dtype=f)).astype(f)
    cos = np.tile(np.cos(angles), (2, 1))
    sin = np.concatenate([-np.sin(angles), np.sin(angles)])
    one = np.stack([np.tile(v, (PART // HD0, 1)) for v in (cos, sin)], axis=1)
    return np.concatenate([one * f(HD0 ** -0.5), one], axis=1).astype(f)


def layout(d):
    f = np.float32

    def columns(v):
        return np.ascontiguousarray(v.reshape(-1, PART).T)

    def ffn(w1, w2):
        one = w1.T.reshape(KD, PART, HIDDEN).transpose(1, 0, 2).reshape(PART, -1)
        two = w2.T.reshape(HT, PART, DIM).transpose(1, 0, 2).reshape(PART, -1)
        return np.concatenate([one, two], axis=1)

    def heads(w, swap=False):
        if swap:
            w = w.reshape(HEADS, 2, HD0 // 2, DIM)[:, ::-1].reshape(DIM, DIM)
        return w.T.reshape(KD, PART, DIM).transpose(1, 0, 2).reshape(PART, -1)

    wq, wk, wv, wo = (d[f"L0_attn_{n}"] for n in ("Wq", "Wk", "Wv", "Wo"))
    stack = wo.T.reshape(GROUP, GROUP, 1, HD0, DIM).repeat(2, axis=2).reshape(GROUP, PART, DIM)
    w_a0 = np.concatenate([heads(wq), heads(wq, True), heads(wk), heads(wk, True), heads(wv),
                           stack.transpose(1, 0, 2).reshape(PART, -1)], axis=1)

    def columns_of(w):
        return w.T.reshape(KD, PART, HD1).transpose(1, 0, 2).reshape(PART, -1)

    wq1, wk1, wv1, wo1 = (d[f"L1_attn_{n}"] for n in ("Wq", "Wk", "Wv", "Wo"))
    groups = []
    for n in range(KV1):
        rows = slice(n * HD1, (n + 1) * HD1)
        mine = [slice((GROUP * n + h) * HD1, (GROUP * n + h + 1) * HD1) for h in range(GROUP)]
        groups.append(np.concatenate([columns_of(wk1[rows]), columns_of(wv1[rows])]
                                     + [columns_of(wq1[r]) for r in mine] + [wo1[:, r].T for r in mine], axis=1))
    w_a1 = np.stack(groups * BATCH)

    return {
        "w_a0": w_a0, "w_a1": w_a1, "rot": rotation(), "mask": np.triu(np.full((PART, PART), MASKED, f), 1),
        "x": np.ascontiguousarray(d["L0_attn_hidden_states"].reshape(TOKENS, DIM)),
        "ident": np.eye(PART, dtype=f),
        "b1": columns(np.concatenate([d["L0_ffn_proj1_bias"][None], d["L1_ffn_B1"]])),
        "gT": columns(d["L1_ffn_LN_G"]), "bT": columns(d["L1_ffn_LN_B"]),
        "rows": np.concatenate([d["L0_ffn_proj2_bias"][None], d["L1_attn_bo"][None], d["L1_ffn_B2"],
                                d["L1_ffn_LN_G"]]),
        "lnb": np.ascontiguousarray(d["L1_ffn_LN_B"]),
        "wffn": np.stack([ffn(d["L0_ffn_proj1"], d["L0_ffn_proj2"])]
                         + [ffn(d["L1_ffn_W1"][i], d["L1_ffn_W2"][i]) for i in range(BLOCKS)]),
    }


def kernel(**inputs):
    import concourse.bacc as bacc
    from concourse.bass_utils import run_bass_kernel_spmd

    arrays = {n: v for n, v in layout({k: np.asarray(v) for k, v in inputs.items()}).items()}
    nc = bacc.Bacc("TRN2", target_bir_lowering=False, num_devices=1)
    aps = {n: nc.dram_tensor(f"in_{n}", v.shape, mybir.dt.from_np(v.dtype), kind="ExternalInput").ap()
           for n, v in arrays.items()}
    aps["out"] = nc.dram_tensor("out", (TOKENS, DIM), mybir.dt.float32, kind="ExternalOutput").ap()
    build(nc, aps)
    r = run_bass_kernel_spmd(nc, [{f"in_{n}": v for n, v in arrays.items()}], core_ids=[0])
    return r.results[0]["out"].reshape(BATCH, SEQ, DIM)
```
